# Optimizing a Trainium2 kernel written in Bass

```python
import numpy as np
import jax
import jax.numpy as jnp

def _softmax(x, axis=-1):
    return jax.nn.softmax(x, axis=axis)

def _gelu(x):
    return jax.nn.gelu(x, approximate=True)

def _silu(x):
    return jax.nn.silu(x)

def _sigmoid(x):
    return jax.nn.sigmoid(x)

def _layernorm(x, axis=-1, eps=1e-05):
    m = jnp.mean(x, axis=axis, keepdims=True)
    v = jnp.var(x, axis=axis, keepdims=True)
    return (x - m) / jnp.sqrt(v + eps)

def _scatter_add(tgt, idx, src, axis=0):
    return tgt.at[idx].add(src)

def _segment_sum(src, seg, n):
    return jax.ops.segment_sum(src, seg, n)
kernel_name = 'mk_flamingo_gated_d2_seqx_r4_f535c4'

def setup_inputs(seed: int=0):
    np.random.seed(seed)
    _w = jnp.asarray

    def _rec_inputs():
        import jax
        import jax.numpy as jnp
        _rk = jax.random.key(seed)
        x = -0.0003929 + 0.9999 * jax.random.normal(jax.random.fold_in(_rk, 1), (8, 512, 256), jnp.float32)
        _lenS = 512 - jax.random.randint(jax.random.fold_in(_rk, 7), (8,), 0, max(1, 512 // 4) + 1, jnp.int32)
        _lenS2 = 1601 - jax.random.randint(jax.random.fold_in(_rk, 8), (8,), 0, max(1, 1601 // 4) + 1, jnp.int32)
        _ctx_1024P = jax.random.normal(jax.random.fold_in(_rk, 11), (8, 16, 256), jnp.float32)
        _ctx_1024c = jax.random.dirichlet(jax.random.fold_in(_rk, 511), 0.3 * jnp.ones((16,), jnp.float32), (8, 1601))
        _ctx_1024t = jnp.einsum('bsk,bkd->bsd', _ctx_1024c, _ctx_1024P)
        _ctx_1024t = _ctx_1024t * jax.lax.rsqrt(jnp.mean(jnp.square(_ctx_1024t)) + 1e-12) * 0.953939
        ctx_1024 = 2.81802e-05 + 1.00001 * (_ctx_1024t + 0.3 * jax.random.normal(jax.random.fold_in(_rk, 611), (8, 1601, 256), jnp.float32))
        _validS = jnp.arange(512)[None, :] < _lenS[:, None]
        _validS2 = jnp.arange(1601)[None, :] < _lenS2[:, None]
        _causal = jnp.tril(jnp.ones((512, 512), dtype=bool))
        mask_BxSxS2_ff0 = jnp.where(jnp.ones((8, 512, 1601), dtype=bool), 0.0, -1000000000.0).astype(jnp.float32)
        mask_1x1xSxS2_if1 = jnp.where(jnp.ones((1, 1, 512, 1601), dtype=bool), 1, 0).astype(jnp.int32)
        _g = jax.random.normal(jax.random.fold_in(_rk, 9001), (2, 2), jnp.float32)
        _g = jnp.sign(_g) * jnp.maximum(jnp.abs(_g), 1.0) + (_g == 0) * 1.0
        g_xattn = _g[0]
        g_ffn = _g[1]
        return (x, ctx_1024, mask_BxSxS2_ff0, mask_1x1xSxS2_if1, g_xattn, g_ffn)
    x, ctx_1024, mask_BxSxS2_ff0, mask_1x1xSxS2_if1, g_xattn, g_ffn = _rec_inputs()

    def _L0_xattn_setup():
        import jax, jax.numpy as jnp
        import numpy as np
        B, L, J, D_MODEL, N_HIDDEN = (8, 512, 512, 256, 256)
        key = jax.random.key(seed)
        ks = jax.random.split(key, 6)
        scale = 1.0 / np.sqrt(D_MODEL)
        return {'q': jax.random.normal(ks[0], (B, L, D_MODEL), dtype=jnp.float32), 'k': jax.random.normal(ks[1], (B, J, D_MODEL), dtype=jnp.float32), 'v': jax.random.normal(ks[2], (B, J, D_MODEL), dtype=jnp.float32), 'mask': jnp.zeros((B, L, J), dtype=jnp.float32), 'W_q': jax.random.normal(ks[3], (N_HIDDEN, D_MODEL), dtype=jnp.float32) * scale, 'W_k': jax.random.normal(ks[4], (N_HIDDEN, D_MODEL), dtype=jnp.float32) * scale, 'W_v': jax.random.normal(ks[5], (N_HIDDEN, D_MODEL), dtype=jnp.float32) * scale}
    _L0_xattn_all = _L0_xattn_setup()
    _L0_xattn_in = {k: v for k, v in _L0_xattn_all.items() if k in ('W_q', 'W_k', 'W_v')}
    del _L0_xattn_all

    def _L0_ffn_setup():
        import jax, jax.numpy as jnp
        import numpy as np
        N_HEAD = 16
        N_ACTIVE = 4
        D_MODEL = 256
        D_ATTN = 64
        B = 4
        S = 512
        key = jax.random.key(seed)
        ks = jax.random.split(key, 6)
        sc = 1.0 / np.sqrt(D_MODEL).astype(np.float32)
        return {'x': jax.random.normal(ks[0], (B, S, D_MODEL), jnp.float32), 'Wq': jax.random.normal(ks[1], (D_MODEL, N_HEAD * D_ATTN), jnp.float32) * sc, 'bq': jnp.zeros((N_HEAD * D_ATTN,), jnp.float32), 'Wk': jax.random.normal(ks[2], (D_MODEL, N_HEAD * D_ATTN), jnp.float32) * sc, 'bk': jnp.zeros((N_HEAD * D_ATTN,), jnp.float32), 'Wv': jax.random.normal(ks[3], (D_MODEL, N_HEAD * D_ATTN), jnp.float32) * sc, 'bv': jnp.zeros((N_HEAD * D_ATTN,), jnp.float32), 'Wr': jax.random.normal(ks[4], (D_MODEL, N_HEAD), jnp.float32) * sc, 'br': jnp.zeros((N_HEAD,), jnp.float32), 'Wo': jax.random.normal(ks[5], (N_ACTIVE * D_ATTN, D_MODEL), jnp.float32) * (1.0 / np.sqrt(N_ACTIVE * D_ATTN).astype(np.float32)), 'bo': jnp.zeros((D_MODEL,), jnp.float32)}
    _L0_ffn_all = _L0_ffn_setup()
    _L0_ffn_in = {k: v for k, v in _L0_ffn_all.items() if k in ('Wq', 'bq', 'Wk', 'bk', 'Wv', 'bv', 'Wr', 'br', 'Wo', 'bo')}
    del _L0_ffn_all

    def _L1_xattn_setup():
        import jax, jax.numpy as jnp
        import numpy as np
        D_MODEL = 256
        HEADS = 16
        D_K = D_MODEL // HEADS
        key = jax.random.key(seed)
        ks = jax.random.split(key, 12)
        B, S = (4, 512)
        s = 1.0 / np.sqrt(D_MODEL)
        return {'q': jax.random.normal(ks[0], (B, S, D_MODEL), jnp.float32), 'k': jax.random.normal(ks[1], (B, S, D_MODEL), jnp.float32), 'v': jax.random.normal(ks[2], (B, S, D_MODEL), jnp.float32), 'mask': jnp.ones((1, 1, S, S), jnp.int32), 'w_q': jax.random.normal(ks[3], (D_MODEL, D_MODEL), jnp.float32) * s, 'b_q': jnp.zeros((D_MODEL,), jnp.float32), 'w_k': jax.random.normal(ks[4], (D_MODEL, D_MODEL), jnp.float32) * s, 'b_k': jnp.zeros((D_MODEL,), jnp.float32), 'w_v': jax.random.normal(ks[5], (D_MODEL, D_MODEL), jnp.float32) * s, 'b_v': jnp.zeros((D_MODEL,), jnp.float32), 'w_o': jax.random.normal(ks[6], (D_MODEL, D_MODEL), jnp.float32) * s, 'b_o': jnp.zeros((D_MODEL,), jnp.float32)}
    _L1_xattn_all = _L1_xattn_setup()
    _L1_xattn_in = {k: v for k, v in _L1_xattn_all.items() if k in ('w_q', 'b_q', 'w_k', 'b_k', 'w_v', 'b_v', 'w_o', 'b_o')}
    del _L1_xattn_all

    def _L1_ffn_setup():
        import jax, jax.numpy as jnp
        import numpy as np
        D_MODEL = 256
        MLP_DIM = 1024
        N_EXPERTS = 8
        B, T = (4, 256)
        key = jax.random.key(seed)
        ks = jax.random.split(key, 7)
        scale_in = (1.0 / D_MODEL) ** 0.5
        scale_out = (1.0 / MLP_DIM) ** 0.5
        bound_g = (1.0 / D_MODEL) ** 0.5
        w_gate = jax.random.uniform(ks[0], (D_MODEL, N_EXPERTS), minval=-bound_g, maxval=bound_g, dtype=jnp.float32)
        b_gate = jax.random.uniform(ks[1], (N_EXPERTS,), minval=-bound_g, maxval=bound_g, dtype=jnp.float32)
        W1 = jax.random.uniform(ks[2], (N_EXPERTS, D_MODEL, MLP_DIM), minval=-scale_in, maxval=scale_in, dtype=jnp.float32)
        b1 = jnp.zeros((N_EXPERTS, MLP_DIM), dtype=jnp.float32)
        W2 = jax.random.uniform(ks[3], (N_EXPERTS, MLP_DIM, D_MODEL), minval=-scale_out, maxval=scale_out, dtype=jnp.float32)
        b2 = jnp.zeros((N_EXPERTS, D_MODEL), dtype=jnp.float32)
        x = jax.random.normal(ks[4], (B, T, D_MODEL), dtype=jnp.float32)
        return {'x': x, 'w_gate': w_gate, 'b_gate': b_gate, 'W1': W1, 'b1': b1, 'W2': W2, 'b2': b2}
    _L1_ffn_all = _L1_ffn_setup()
    _L1_ffn_in = {k: v for k, v in _L1_ffn_all.items() if k in ('w_gate', 'b_gate', 'W1', 'b1', 'W2', 'b2')}
    del _L1_ffn_all
    return {'x': x, 'ctx_1024': ctx_1024, 'mask_BxSxS2_ff0': mask_BxSxS2_ff0, 'mask_1x1xSxS2_if1': mask_1x1xSxS2_if1, 'g_xattn': g_xattn, 'g_ffn': g_ffn, 'L0_xattn_W_q': _L0_xattn_in['W_q'], 'L0_xattn_W_k': _L0_xattn_in['W_k'], 'L0_xattn_W_v': _L0_xattn_in['W_v'], 'L0_ffn_Wq': _L0_ffn_in['Wq'], 'L0_ffn_bq': _L0_ffn_in['bq'], 'L0_ffn_Wk': _L0_ffn_in['Wk'], 'L0_ffn_bk': _L0_ffn_in['bk'], 'L0_ffn_Wv': _L0_ffn_in['Wv'], 'L0_ffn_bv': _L0_ffn_in['bv'], 'L0_ffn_Wr': _L0_ffn_in['Wr'], 'L0_ffn_br': _L0_ffn_in['br'], 'L0_ffn_Wo': _L0_ffn_in['Wo'], 'L0_ffn_bo': _L0_ffn_in['bo'], 'L1_xattn_w_q': _L1_xattn_in['w_q'], 'L1_xattn_b_q': _L1_xattn_in['b_q'], 'L1_xattn_w_k': _L1_xattn_in['w_k'], 'L1_xattn_b_k': _L1_xattn_in['b_k'], 'L1_xattn_w_v': _L1_xattn_in['w_v'], 'L1_xattn_b_v': _L1_xattn_in['b_v'], 'L1_xattn_w_o': _L1_xattn_in['w_o'], 'L1_xattn_b_o': _L1_xattn_in['b_o'], 'L1_ffn_w_gate': _L1_ffn_in['w_gate'], 'L1_ffn_b_gate': _L1_ffn_in['b_gate'], 'L1_ffn_W1': _L1_ffn_in['W1'], 'L1_ffn_b1': _L1_ffn_in['b1'], 'L1_ffn_W2': _L1_ffn_in['W2'], 'L1_ffn_b2': _L1_ffn_in['b2']}

def reference(x, ctx_1024, mask_BxSxS2_ff0, mask_1x1xSxS2_if1, g_xattn, g_ffn, L0_xattn_W_q, L0_xattn_W_k, L0_xattn_W_v, L0_ffn_Wq, L0_ffn_bq, L0_ffn_Wk, L0_ffn_bk, L0_ffn_Wv, L0_ffn_bv, L0_ffn_Wr, L0_ffn_br, L0_ffn_Wo, L0_ffn_bo, L1_xattn_w_q, L1_xattn_b_q, L1_xattn_w_k, L1_xattn_b_k, L1_xattn_w_v, L1_xattn_b_v, L1_xattn_w_o, L1_xattn_b_o, L1_ffn_w_gate, L1_ffn_b_gate, L1_ffn_W1, L1_ffn_b1, L1_ffn_W2, L1_ffn_b2):
    import jax
    import jax.numpy as jnp

    def _L0_xattn_ref(q, k, v, mask, W_q, W_k, W_v):
        import jax, jax.numpy as jnp
        import numpy as np
        B, L, J, D_MODEL, N_HIDDEN = (8, 512, 512, 256, 256)
        qp = jnp.einsum('bld,hd->blh', q, W_q)
        kp = jnp.einsum('bjd,hd->bjh', k, W_k)
        vp = jnp.einsum('bjd,hd->bjh', v, W_v)
        scores = jnp.einsum('blh,bjh->blj', qp, kp) / jnp.sqrt(jnp.float32(N_HIDDEN)).astype(qp.dtype)
        scores = scores + mask
        attn = jax.nn.softmax(scores, axis=-1)
        return jnp.einsum('blj,bjh->blh', attn, vp)

    def _L0_ffn_ref(x, Wq, bq, Wk, bk, Wv, bv, Wr, br, Wo, bo):
        import jax, jax.numpy as jnp
        import numpy as np
        N_HEAD = 16
        N_ACTIVE = 4
        D_MODEL = 256
        D_ATTN = 64
        B = 4
        S = 512
        b, s, _ = x.shape
        dist = jax.nn.softmax(jnp.mean(x @ Wr + br, axis=1), axis=-1)
        _, idx = jax.lax.top_k(dist, N_ACTIVE)
        idx = jnp.sort(idx, axis=-1)

        def proj(W, bias):
            return (x @ W + bias).reshape(b, s, N_HEAD, D_ATTN).transpose(0, 2, 1, 3)
        Q = proj(Wq, bq)
        K = proj(Wk, bk)
        V = proj(Wv, bv)
        gather = lambda t: jnp.take_along_axis(t, idx[:, :, None, None], axis=1)
        Qs, Ks, Vs = (gather(Q), gather(K), gather(V))
        scale = 1.0 / jnp.sqrt(jnp.asarray(D_ATTN, x.dtype))
        score = jax.nn.softmax(jnp.einsum('bhqd,bhkd->bhqk', Qs, Ks) * scale, axis=-1)
        O = jnp.einsum('bhqk,bhkd->bhqd', score, Vs)
        O = O.transpose(0, 2, 1, 3).reshape(b, s, N_ACTIVE * D_ATTN)
        return O @ Wo + bo

    def _L1_xattn_ref(q, k, v, mask, w_q, b_q, w_k, b_k, w_v, b_v, w_o, b_o):
        import jax, jax.numpy as jnp
        import numpy as np
        D_MODEL = 256
        HEADS = 16
        D_K = D_MODEL // HEADS
        B, S, _ = q.shape

        def split_heads(x):
            return x.reshape(B, -1, HEADS, D_K).transpose(0, 2, 1, 3)
        query = split_heads(q @ w_q.T + b_q)
        key = split_heads(k @ w_k.T + b_k)
        value = split_heads(v @ w_v.T + b_v)
        scores = jnp.einsum('bhqd,bhkd->bhqk', query, key) / np.sqrt(D_K)
        scores = jnp.where(mask == 0, jnp.float32(-1000000000.0), scores)
        attn = jax.nn.softmax(scores, axis=-1)
        x = jnp.einsum('bhqk,bhkd->bhqd', attn, value)
        x = x.transpose(0, 2, 1, 3).reshape(B, S, D_MODEL)
        return x @ w_o.T + b_o

    def _L1_ffn_ref(x, w_gate, b_gate, W1, b1, W2, b2):
        import jax, jax.numpy as jnp
        import numpy as np
        D_MODEL = 256
        MLP_DIM = 1024
        N_EXPERTS = 8
        B, T = (4, 256)
        b, t, d = x.shape
        x_flat = x.reshape(b * t, d)
        logits = x_flat @ w_gate + b_gate
        probs = jax.nn.softmax(logits, axis=-1)
        route_p = jnp.max(probs, axis=-1)
        route_idx = jnp.argmax(probs, axis=-1)
        h = jnp.einsum('nd,edm->enm', x_flat, W1) + b1[:, None, :]
        h = jax.nn.relu(h)
        y = jnp.einsum('enm,emd->end', h, W2) + b2[:, None, :]
        n = b * t
        out = y[route_idx, jnp.arange(n)] * route_p[:, None]
        return out.reshape(b, t, d)
    x = x + jnp.tanh(g_xattn[0]) * _L0_xattn_ref(_layernorm(x, axis=-1), ctx_1024, ctx_1024, mask_BxSxS2_ff0, L0_xattn_W_q, L0_xattn_W_k, L0_xattn_W_v)
    x = x + jnp.tanh(g_ffn[0]) * _L0_ffn_ref(_layernorm(x, axis=-1), L0_ffn_Wq, L0_ffn_bq, L0_ffn_Wk, L0_ffn_bk, L0_ffn_Wv, L0_ffn_bv, L0_ffn_Wr, L0_ffn_br, L0_ffn_Wo, L0_ffn_bo)
    x = x + jnp.tanh(g_xattn[1]) * _L1_xattn_ref(_layernorm(x, axis=-1), ctx_1024, ctx_1024, mask_1x1xSxS2_if1, L1_xattn_w_q, L1_xattn_b_q, L1_xattn_w_k, L1_xattn_b_k, L1_xattn_w_v, L1_xattn_b_v, L1_xattn_w_o, L1_xattn_b_o)
    x = x + jnp.tanh(g_ffn[1]) * _L1_ffn_ref(_layernorm(x, axis=-1), L1_ffn_w_gate, L1_ffn_b_gate, L1_ffn_W1, L1_ffn_b1, L1_ffn_W2, L1_ffn_b2)
    return x

_drawn_inputs = setup_inputs


def setup_inputs(seed=0):
    import zlib

    import numpy as np

    out = dict(_drawn_inputs(seed))
    spreads = {'g_ffn': (-1.0, 0.6),
     'L0_ffn_bq': (0.0, 0.8),
     'L0_ffn_bk': (0.0, 0.8),
     'L0_ffn_bv': (0.0, 0.1),
     'L0_ffn_br': (0.0, 0.1),
     'L0_ffn_bo': (0.0, 0.1),
     'L1_xattn_b_q': (0.0, 0.449),
     'L1_xattn_b_k': (0.0, 0.8),
     'L1_xattn_b_v': (0.0, 0.1),
     'L1_xattn_b_o': (0.0, 0.1),
     'L1_ffn_b1': (0.0, 0.8),
     'L1_ffn_b2': (0.0, 0.454)}
    factors = {'L1_ffn_b_gate': 6.312}
    for name, (base, spread) in spreads.items():
        noise = np.random.default_rng([zlib.crc32(name.encode()), seed]).standard_normal(out[name].shape)
        drawn = base * np.exp(spread * noise) if base else spread * noise
        out[name] = jnp.asarray(drawn.astype(out[name].dtype))
    for name, factor in factors.items():
        out[name] = (out[name] * factor).astype(out[name].dtype)
    return out
```

```python
from contextlib import ExitStack

import numpy as np

import concourse.bass as bass
from concourse import mybir
from concourse.bass import IndirectOffsetOnAxis

F32 = mybir.dt.float32
BF16 = mybir.dt.bfloat16
I32 = mybir.dt.int32
U32 = mybir.dt.uint32
ALU = mybir.AluOpType
ACT = mybir.ActivationFunctionType
AX = mybir.AxisListType

B, S, C, D = 8, 512, 1601, 256
P = 128
QT = S // P
KD = D // P
CT = -(-C // P)
CL = C - (CT - 1) * P
EPS = 1e-5
A_CH = [(0, 512), (512, 512), (1024, 512), (1536, C - 1536)]
K_CH = [(0, 384), (384, 384), (768, 384), (1152, C - 1152)]
NCH = 4
M_N = -(-C // NCH)
M_CH = [(0, M_N - 1), (M_N - 1, M_N - 1), (2 * M_N - 2, M_N), (C - M_N, M_N)]
HB, DB, ACTIVE = 16, 64, 4
HC, DC = 16, 16
GH = 4
NG = HC // GH
KPART = (0, 1, 0, 2, 0, 1)
QPART = (0, 0, 1, 0, 2, 1)
NR = len(KPART)
ROWS = NR * DC
STK = ROWS + 3
CMAX = max(n for _, n in K_CH)
NS_C = GH * QT * NCH // 2
LEAD = 8
VP = -(-CT // 2)
UN = CT * GH
MT_AT = UN - 8
RING = 8
NE, FF = 8, 1024
FM = FF // P
TOK = B * S
NT = TOK // P
TS = 256
ET = TOK // TS + NE
MASKED = -float(2.0 ** 100)


class Ticks:

    def __init__(self, sem):
        self.sem, self.base, self.n = sem, 0, 0

    def tick(self):
        self.n += 1
        return self.sem, 1

    def now(self):
        return self.base + self.n


def bank_m(g):
    return 5 + ((g - 1) * UN + MT_AT) % 3 if g else 6


def rows(c):
    return P if c < CT - 1 else CL


def loads_before(b, g, each, ones):
    per_batch = 16 * (each * (2 if g % 3 == 0 else 1) + ones)
    return per_batch * b + 16 * (each * (g // 3 + 1) + ones)


def flamingo(nc, a):
    ctx_stack = ExitStack()
    with ctx_stack:
        def sem(name):
            return ctx_stack.enter_context(nc.semaphore(name))

        def sb(name, shape, dt):
            return ctx_stack.enter_context(nc.sbuf_tensor(name, shape, dt))

        NPS = 8
        PS = ctx_stack.enter_context(nc.psum_tensor("PS", [P, NPS, 512], F32))

        ident = sb("ident", [P, P], F32)
        identb = sb("identb", [P, P], BF16)
        gA = sb("gA", [P, KD, D], F32)
        wvA = sb("wvA", [P, KD, D], F32)
        woB = sb("woB", [P, KD, D], F32)
        wrB = sb("wrB", [P, KD, HB], F32)
        brB = sb("brB", [1, HB], F32)
        wqC = sb("wqC", [P, KD, D], F32)
        wkC = sb("wkC", [P, KD, D], F32)
        wvC = sb("wvC", [P, KD, D], F32)
        woC = sb("woC", [P, KD, D], F32)
        bqC = sb("bqC", [P, KD], F32)
        bkC = sb("bkC", [P, KD], F32)
        bvC = sb("bvC", [P, D], F32)
        boB = sb("boB", [P, D], F32)
        boC = sb("boC", [P, D], F32)
        wgD = sb("wgD", [P, KD, NE], F32)
        bgD = sb("bgD", [P, NE], F32)
        tg = sb("tg", [P, 4], F32)
        mhalf = sb("mhalf", [P, QT], F32)
        maskT = sb("maskT", [P, CT, S], BF16)
        mflag = sb("mflag", [P, 2], I32)
        expert = sb("expert", [P, NT], F32)
        weight = sb("weight", [P, NT], F32)

        xin = sb("xin", [P, QT, D], F32)
        xw = sb("xw", [P, QT, D], F32)
        xn = sb("xn", [P, QT, D], F32)
        xT = sb("xT", [P, KD, S], F32)
        ctxN = sb("ctxN", [P, CT, D], F32)
        ctxT = sb("ctxT", [P, KD, C], F32)
        mk = [sb(f"mk{i}", [P, C], F32) for i in range(2)]
        vc = sb("vc", [P, CT, HC, DC + 1], F32)
        ws = sb("ws", [P, 3, KD, ACTIVE, DB], F32)
        bs = sb("bs", [P, 2, 3], F32)
        st = sb("st", [P, QT, 6], F32)
        mv = sb("mv", [P, QT, 2], F32)
        vpe = sb("vpe", [P, QT], F32)
        rstd = sb("rstd", [P, QT], F32)
        small = sb("small", [P, 64], F32)
        mxA, nmA, rsA, rcA = (small[:, 0:4], small[:, 4:8], small[:, 8:12], small[:, 12:16])
        msum = small[:, 16:18]
        rt = sb("rt", [1, 8, HB], F32)
        rti = sb("rti", [1, 2, 8], U32)
        nmB = sb("nmB", [P, ACTIVE * QT], F32)
        rsB = sb("rsB", [P, ACTIVE * QT], F32)
        mxC = sb("mxC", [P, GH, QT, NCH // 2], F32)
        nmC = sb("nmC", [P, QT, GH], F32)
        nmr = sb("nmr", [P, QT, GH], F32)
        npt = sb("npt", [P, QT, 3, GH], BF16)
        mrow = sb("mrow", [3 * GH, S], BF16)
        rcC = sb("rcC", [P, QT, GH], F32)
        lg = sb("lg", [P, QT, NE], F32)
        lgd = sb("lgd", [P, QT, NE], F32)
        mx8 = sb("mx8", [P, QT, 8], F32)
        ix8 = sb("ix8", [P, QT, 8], U32)
        ssum = sb("ssum", [P, QT], F32)

        def carve(region, size):
            at = [0]

            def take(dims, dt, parts=P):
                n = int(np.prod(dims)) * (4 if dt in (F32, I32, U32) else 2)
                words = -(-n // 4)
                ap = region[0:parts, at[0]:at[0] + words]
                at[0] += words
                assert at[0] <= size, (at[0], size)
                if dt is not F32:
                    ap = ap.bitcast(dt)
                if dt in (BF16,) and words * 2 != int(np.prod(dims)):
                    ap = ap[:, 0:int(np.prod(dims))]
                names = "abcd"[:len(dims)]
                if len(dims) > 1:
                    ap = ap.rearrange(f"p ({' '.join(names)}) -> p {' '.join(names)}",
                                      **{k: v for k, v in zip(names, dims)})
                return ap
            return take

        R1, R2 = 11910, 12700
        reg1 = sb("reg1", [P, R1], F32)
        reg2 = sb("reg2", [P, R2], F32)

        take = carve(reg1, R1)
        eA = [take([C], F32) for _ in range(2)]
        ptA = take([CT, S], F32)
        qgA = take([KD, S], F32)
        otA = take([KD, S], F32)
        take = carve(reg1, R1)
        pr = [take([S], F32) for _ in range(RING)]
        oc = [take([S], F32) for _ in range(2)]
        ao = take([QT, D], F32)
        aoT = take([KD, S], F32)
        kr = [take([CMAX], F32) for _ in range(4)]
        kp = [take([3, CMAX + 1], BF16) for _ in range(4)]
        take = carve(reg2, R2)
        qB = take([2, S], F32)
        kB = take([2, S], F32)
        pB = [take([S], F32) for _ in range(4)]
        ptB = [take([QT, S], F32) for _ in range(2)]
        oB = take([2, S], F32)
        vB = take([QT, ACTIVE * DB], F32)
        take = carve(reg2, R2)
        ks = [take([GH, C], BF16) for _ in range(3)]
        qs = [take([GH, S], BF16) for _ in range(3)]
        tq = ctxN[:, 0:4, :].rearrange("p a b -> p (a b)").rearrange("p (m q) -> p m q", m=KD)
        qp = ctxN[:, 4:10, :].rearrange("p a b -> p (a b)").bitcast(BF16)[:, 0:3 * KD * S].rearrange(
            "p (r m q) -> p r m q", r=3, m=KD)

        take = carve(reg2, R2)
        w1 = [take([KD, FF], F32) for _ in range(2)]
        w2 = [take([FM, D], F32) for _ in range(2)]
        b1 = [take([FM], F32) for _ in range(2)]
        b2 = [take([D], F32) for _ in range(2)]
        xs = [take([2, D], F32) for _ in range(2)]
        xsT = [take([KD, TS], F32) for _ in range(2)]
        take = carve(reg1, R1)
        big = take([NT, D], F32)
        hT = take([FM, TS], F32)
        ys = [take([2, D], F32) for _ in range(2)]
        take = carve(vc[:, :, :, :].rearrange("p a b c -> p (a b c)"), CT * HC * (DC + 1))
        oh = take([NT, NE], F32)
        tot = take([NT, NE], F32)
        inc = [take([NT, NE], F32) for _ in range(2)]
        lt = take([P], F32)
        onesD = take([P], F32)
        ncount = take([NE], F32)
        cmp = take([NE, NE * 2], F32)
        tiles = take([NE], F32)
        tinc = [take([NE], F32) for _ in range(2)]
        tbase = take([NE], F32)
        slotf = take([NT], F32)
        slot = take([NT], I32)
        iota_e = take([NE], F32)
        iota_k = take([NE * 2], F32)
        iota_t = take([ET], F32)
        tcmp = take([ET, NE], F32)
        texf = take([ET], F32)
        tex = take([ET], I32)
        assert NE * 2 == TOK // TS
        fin = [ctxN[:, 0:4, :], ctxN[:, 4:8, :]]

        dramK = nc.dram_tensor("dramK", (3, D, C), BF16, kind="Internal").ap()
        dramQ = nc.dram_tensor("dramQ", (3, D, S), BF16, kind="Internal").ap()
        dramX = nc.dram_tensor("dramX", (B, P, QT, D), F32, kind="Internal").ap()
        dramN = nc.dram_tensor("dramN", (B, P, QT, D), F32, kind="Internal").ap()
        dramS = nc.dram_tensor("dramS", (ET * TS, D), F32, kind="Internal").ap()
        dramY = nc.dram_tensor("dramY", (ET * TS, D), F32, kind="Internal").ap()

        ld = {n: sem("ld_" + n) for n in ("w", "g", "x", "ctxN", "ctxT", "mk0", "mk1", "ws", "mT")}
        kd_stored = [sem(f"kd_stored{i}") for i in range(NCH)]
        qd_stored = sem("qd_stored")
        ks_loaded = [sem(f"ks_loaded{i}") for i in range(3)]
        qs_loaded = [sem(f"qs_loaded{i}") for i in range(3)]
        m_loaded = sem("m_loaded")
        x_stored, n_stored, s_zeroed = sem("x_stored"), sem("n_stored"), sem("s_zeroed")
        N = {}

        def counted(name, per_batch):
            N[name] = per_batch
            return sem(name)

        v_var = counted("v_var", 4)
        g_rstd = counted("g_rstd", 4)
        v_xn = counted("v_xn", 16)
        pe_xT = counted("pe_xT", 4)
        a_xT = counted("a_xT", 4)
        v_xT = counted("v_xT", 4)
        pe_qg = counted("pe_qg", 2)
        a_qg = counted("a_qg", 1)
        v_qg = counted("v_qg", 1)
        pe_sA = counted("pe_sA", 16)
        v_ttr = counted("v_ttr", 16)
        v_nmA = counted("v_nmA", 4)
        a_expA = counted("a_expA", 4)
        pe_ptA = counted("pe_ptA", 4)
        a_ptA = counted("a_ptA", 4)
        v_ptA = counted("v_ptA", 4)
        pe_otA = counted("pe_otA", 2)
        a_otA = counted("a_otA", 1)
        v_otA = counted("v_otA", 1)
        pe_oA = counted("pe_oA", 4)
        v_oA = counted("v_oA", 4)
        v_ms = counted("v_ms", 1)
        pe_rl = counted("pe_rl", 1)
        v_rm = counted("v_rm", 1)
        a_re = counted("a_re", 1)
        v_idx = counted("v_idx", 1)
        pe_kp = counted("pe_kp", 8)
        a_kh = counted("a_kh", 8)
        v_kr = counted("v_kr", 8)
        g_ks = counted("g_ks", 8)
        pe_qkvB = counted("pe_qkvB", 6)
        a_kB = counted("a_kB", 2)
        v_qB = counted("v_qB", 2)
        a_vB = counted("a_vB", 1)
        v_vB = counted("v_vB", 1)
        pe_sB = counted("pe_sB", 16)
        v_nmB = counted("v_nmB", 16)
        a_expB = counted("a_expB", 16)
        v_pB = counted("v_pB", 16)
        pe_tB = counted("pe_tB", 16)
        a_ptB = counted("a_ptB", 16)
        pe_pvB = counted("pe_pvB", 4)
        v_otB = counted("v_otB", 2)
        pe_oB = counted("pe_oB", 4)
        v_oB = counted("v_oB", 4)
        pe_qC = counted("pe_qC", 2)
        v_tq = counted("v_tq", 1)
        a_qh = counted("a_qh", 1)
        v_qs = counted("v_qs", 1)
        pe_vp = counted("pe_vp", VP)
        a_vp = counted("a_vp", VP)
        pe_sC = counted("pe_sC", NG * NS_C)
        v_mx = counted("v_mx", NG * NS_C)
        v_np = counted("v_np", NG)
        pe_mT = counted("pe_mT", NG)
        a_mrow = counted("a_mrow", NG)
        pe_st = counted("pe_st", NG * UN)
        a_expC = counted("a_expC", NG * UN)
        pe_pv = counted("pe_pv", NG * CT)
        a_oc = counted("a_oc", NG)
        pe_oT = counted("pe_oT", NG)
        v_ao = counted("v_ao", NG)
        v_ab = counted("v_ab", 1)
        pe_aT = counted("pe_aT", 2)
        a_aT = counted("a_aT", 1)
        v_aT = counted("v_aT", 1)
        pe_oC = counted("pe_oC", 4)
        v_oC = counted("v_oC", 4)
        pe_gate = counted("pe_gate", 1)
        v_gd = counted("v_gd", 1)
        a_ge = counted("a_ge", 1)
        v_self, a_self, g_self = sem("v_self"), sem("a_self"), sem("g_self")
        g_set, v_set, pe_set, a_set = sem("g_set"), sem("v_set"), sem("pe_set"), sem("a_set")
        v_oh, pe_rank, v_slot, v_tex = sem("v_oh"), sem("pe_rank"), sem("v_slot"), sem("v_tex")
        big_loaded, scattered, gathered = sem("big_loaded"), sem("scattered"), [sem(f"gathered{i}") for i in range(B)]
        w_loaded = [sem(f"w_loaded{i}") for i in range(2)]
        xs_loaded = [sem(f"xs_loaded{i}") for i in range(2)]
        pe_xsT, v_xsT, pe_h, a_h, pe_y, v_y = (sem(n) for n in ("pe_xsT", "v_xsT", "pe_h", "a_h", "pe_y", "v_y"))
        ys_stored = [sem(f"ys_stored{i}") for i in range(2)]
        xr_loaded = [sem(f"xr_loaded{i}") for i in range(2)]
        v_out, out_stored = sem("v_out"), sem("out_stored")

        V_SET, V_PER = 6, 118
        NW = 18

        block = ctx_stack.enter_context(nc.Block())

        @block.sync
        def _(sp):
            k2 = "(k p) n -> p k n"
            for dst, src in (
                    (wvA[:], a["A_WvT"].rearrange(k2, p=P)), (woB[:], a["B_Wo"].rearrange(k2, p=P)),
                    (wrB[:], a["B_Wr"].rearrange(k2, p=P)), (brB[:], a["B_br"]),
                    (wqC[:], a["C_WqT"].rearrange(k2, p=P)), (wkC[:], a["C_WkT"].rearrange(k2, p=P)),
                    (wvC[:], a["C_WvT"].rearrange(k2, p=P)), (woC[:], a["C_WoT"].rearrange(k2, p=P)),
                    (bqC[:], a["C_bq"]), (bkC[:], a["C_bk"]),
                    (bvC[:], a["C_bv"].partition_broadcast(P)), (boB[:], a["B_bo"].partition_broadcast(P)),
                    (boC[:], a["C_bo"].partition_broadcast(P)),
                    (wgD[:], a["D_wg"].rearrange(k2, p=P)), (bgD[:], a["D_bg"].partition_broadcast(P)),
                    (tg[:, 0:2], a["g_x"].partition_broadcast(P)),
                    (tg[:, 2:4], a["g_f"].partition_broadcast(P)),
                    (qgA, a["A_WqWk"].rearrange(k2, p=P))):
                sp.dma_start(dst, src).then_inc(ld["w"], 16)
            mraw = ptA.bitcast(I32)
            sp.dma_start(mraw[:, 0:CT - 1, :],
                         a["C_maskT"][0:(CT - 1) * P, :].rearrange("(c p) q -> p c q", p=P)).then_inc(ld["mT"], 16)
            sp.dma_start(mraw[0:CL, CT - 1, :], a["C_maskT"][(CT - 1) * P:C, :]).then_inc(ld["mT"], 16)
            sp.wait_ge(g_set, 4)
            for i in range(ET * TS // (P * 8)):
                sp.dma_start(dramS[i * P * 8:(i + 1) * P * 8, :].rearrange("(p r) n -> p r n", p=P),
                             reg2[:, 0:8 * D].rearrange("p (r n) -> p r n", r=8)).then_inc(s_zeroed, 16)
            sp.wait_ge(s_zeroed, 16 * (ET * TS // (P * 8)))

            with sp.Fori(0, B) as b:
                sp.wait_ge(v_idx, b + 1)
                sp.nop(nofuse=True)
                for j in range(ACTIVE):
                    h = sp.value_load(rti[0:1, 1, j:j + 1], min_val=0, max_val=HB - 1)
                    sp.dma_start(ws[:, :, :, j, :], a["B_w"][bass.ds(h, 1)].rearrange("o p m k n -> (o p) m k n")
                                 ).then_inc(ld["ws"], 16)
                    q = DB * (j % 2)
                    sp.dma_start(bs[q:q + DB, j // 2, :],
                                 a["B_b"][bass.ds(h, 1)].rearrange("o p m -> (o p) m")).then_inc(ld["ws"], 16)

                def store_k(u):
                    m, (c0, n) = u // NCH, K_CH[u % NCH]
                    sp.wait_ge(g_ks, 8 * b + u + 1)
                    sp.dma_start(dramK[:, m * P:(m + 1) * P, c0:c0 + n].rearrange("r p c -> p r c"),
                                 kp[u % 4][:, :, 0:n]).then_inc(kd_stored[u % 4], 16)

                def load_k(g):
                    for r, part in enumerate(KPART):
                        sp.dma_start(ks[g % 3][r * DC:(r + 1) * DC, :, :],
                                     dramK[part, g * GH * DC:(g + 1) * GH * DC, :].rearrange(
                                         "(h d) c -> d h c", d=DC)).then_inc(ks_loaded[g % 3], 16)

                def load_q(g):
                    for r, part in enumerate(QPART):
                        sp.dma_start(qs[g % 3][r * DC:(r + 1) * DC, :, :],
                                     dramQ[part, g * GH * DC:(g + 1) * GH * DC, :].rearrange(
                                         "(h d) q -> d h q", d=DC)).then_inc(qs_loaded[g % 3], 16)

                for u in range(NCH):
                    store_k(u)
                sp.wait_ge(v_oB, QT * b + QT)
                for i in range(3):
                    sp.dma_start(ks[i][ROWS:STK, :, :], a["ones"].rearrange("r (h c) -> r h c", h=GH)
                                 ).then_inc(ks_loaded[i], 16)
                for i in range(NCH):
                    sp.wait_ge(kd_stored[i], 32 * b + 16)
                load_k(0)
                load_k(1)
                sp.wait_ge(v_qs, b + 1)
                for m in range(KD):
                    sp.dma_start(dramQ[:, m * P:(m + 1) * P, :].rearrange("r p q -> p r q"),
                                 qp[:, :, m, :]).then_inc(qd_stored, 16)
                sp.wait_ge(qd_stored, 16 * KD * (b + 1))
                for g in range(3):
                    load_q(g)
                for u in range(NCH, 2 * NCH):
                    store_k(u)
                for i in range(NCH):
                    sp.wait_ge(kd_stored[i], 32 * b + 32)
                load_k(2)
                for g in range(NG):
                    sp.wait_ge(a_mrow, NG * b + g + 1)
                    for r in range(3):
                        sp.dma_start(qs[g % 3][ROWS + r:ROWS + r + 1, :, :],
                                     mrow[r * GH:(r + 1) * GH, :]).then_inc(m_loaded, 16)
                    if g == 1:
                        sp.wait_ge(pe_pv, CT * NG * b + CT)
                        load_q(3)
                        load_k(3)
                sp.wait_ge(v_oC, QT * b + QT)
                sp.dma_start(dramX[bass.ds(b, 1)].rearrange("o p t n -> (o p) t n"), xw[:]).then_inc(x_stored, 16)
                sp.wait_ge(v_xn, 4 * QT * b + 4 * QT)
                sp.dma_start(dramN[bass.ds(b, 1)].rearrange("o p t n -> (o p) t n"), xn[:]).then_inc(n_stored, 16)

            sp.wait_ge(n_stored, 16 * B)
            sp.wait_ge(x_stored, 16 * B)
            sp.wait_ge(v_gd, B)
            sp.dma_start(big.rearrange("p (b t) n -> p b t n", b=B), dramN.rearrange("b p t n -> p b t n")
                         ).then_inc(big_loaded, 16)
            sp.wait_ge(v_tex, 1)

            def load_weights(j, par):
                e = sp.value_load(tex[0:1, bass.ds(j, 1)], min_val=0, max_val=NE - 1)
                sp.dma_start(w1[par], a["D_W1"][bass.ds(e, 1)].rearrange("o (k p) f -> p (o k) f", p=P)
                             ).then_inc(w_loaded[par], 16)
                sp.dma_start(w2[par], a["D_W2"][bass.ds(e, 1)].rearrange("o (k p) n -> p (o k) n", p=P)
                             ).then_inc(w_loaded[par], 16)
                sp.dma_start(b1[par], a["D_b1"][bass.ds(e, 1)].rearrange("o p m -> (o p) m")
                             ).then_inc(w_loaded[par], 16)
                sp.dma_start(b2[par], a["D_b2"][bass.ds(e, 1)].rearrange("o n -> (o n)").partition_broadcast(P)
                             ).then_inc(w_loaded[par], 16)

            def load_rows(j, par):
                sp.dma_start(xs[par], dramS[bass.ds(TS * j, TS), :].rearrange("(t p) n -> p t n", p=P)
                             ).then_inc(xs_loaded[par], 16)

            def store_rows(j, par):
                sp.wait_ge(v_y, 2 * j + 2)
                sp.dma_start(dramY[bass.ds(TS * j, TS), :].rearrange("(t p) n -> p t n", p=P),
                             ys[par]).then_inc(ys_stored[par], 16)

            load_weights(0, 0)
            load_weights(1, 1)
            sp.wait_ge(scattered, 16 * NT)
            load_rows(0, 0)
            load_rows(1, 1)
            with sp.Fori(0, ET // 2 - 1) as jj:
                for par in range(2):
                    store_rows(2 * jj + par, par)
                    load_rows(2 * jj + par + 2, par)
                    load_weights(2 * jj + par + 2, par)
            for par in range(2):
                store_rows(ET - 2 + par, par)
            for b in range(B + 1):
                if b >= 1:
                    sp.wait_ge(v_out, QT * b)
                    sp.dma_start(a["out"][b - 1].rearrange("(t p) n -> p t n", p=P),
                                 big[:, QT * (b - 1):QT * b, :]).then_inc(out_stored, 16)
                if b < B:
                    sp.dma_start(fin[b % 2], dramX[b]).then_inc(xr_loaded[b % 2], 16)
            sp.wait_ge(out_stored, 16 * B)

        @block.gpsimd
        def _(pool):
            pool.memset(ident[:], 0.0).then_inc(g_set, 1)
            pool.memset(identb[:], 0.0).then_inc(g_set, 1)
            pool.memset(reg2[:, 0:8 * D], 0.0).then_inc(g_set, 1)
            pool.memset(mhalf[:], -0.5).then_inc(g_set, 1)
            pool.wait_ge(g_set, 4)
            for m in (ident, identb):
                pool.affine_select(out=m[:], in_=m[:], compare_op=ALU.not_equal, fill=1.0, base=0,
                                   pattern=[[-1, P]], channel_multiplier=1).then_inc(g_set, 1)
            pool.memset(vc[:, :, :, DC:DC + 1], 1.0).then_inc(g_set, 1)
            pool.wait_ge(v_set, 3)
            pool.partition_all_reduce(small[:, 32:33], small[:, 20:21], P,
                                      bass.bass_isa.ReduceOp.max).then_inc(g_set, 1)

            def load_x(b):
                pool.dma_start(xin[:], a["x"][bass.ds(b, 1)].rearrange("o (t p) n -> p (o t) n", p=P)
                               ).then_inc(ld["x"], 16)

            def load_ctx(b):
                src = a["ctx"][bass.ds(b, 1)].rearrange("o c n -> (o c) n")
                pool.dma_start(ctxN[:, 0:CT - 1, :], src[0:(CT - 1) * P, :].rearrange("(c p) n -> p c n", p=P)
                               ).then_inc(ld["ctxN"], 16)
                pool.dma_start(ctxN[0:CL, CT - 1, :], src[(CT - 1) * P:C, :]).then_inc(ld["ctxN"], 16)

            def load_ctxT(b):
                pool.dma_start(ctxT[:], a["ctxT"][bass.ds(b, 1)].rearrange("o (k p) c -> p (o k) c", p=P)
                               ).then_inc(ld["ctxT"], 16)

            def load_mask(b, t):
                src = a["A_mask"][bass.ds(b, 1)].rearrange("o q c -> (o q) c")
                pool.dma_start(mk[t % 2][:], src[t * P:(t + 1) * P, :]).then_inc(ld[f"mk{t % 2}"], 16)

            load_x(0)
            load_ctxT(0)
            load_mask(0, 0)
            load_mask(0, 1)
            load_ctx(0)

            def root(ln):
                pool.wait_ge(v_var, 4 * b + ln + 1)
                pool.tensor_tensor(rstd[:], vpe[:], mhalf[:], ALU.pow).then_inc(g_rstd, 1)

            def split_k(u):
                n = K_CH[u % NCH][1]
                pool.wait_ge(v_kr, 8 * b + u + 1)
                pool.nop(nofuse=True)
                pool.tensor_copy(kp[u % 4][:, 1, 0:n], kr[u % 4][:, 0:n]).then_inc(g_self, 1)
                pool.wait_ge(g_self, 8 * b + u + 1)
                pool.tensor_tensor(kp[u % 4][:, 2, 0:n], kr[u % 4][:, 0:n], kp[u % 4][:, 1, 0:n],
                                   ALU.subtract).then_inc(g_ks, 1)

            with pool.Fori(0, B) as b:
                root(0)
                for t in range(2, QT):
                    pool.wait_ge(v_ttr, NCH * QT * b + NCH * (t - 1))
                    load_mask(b, t)
                with pool.If(b < B - 1):
                    for t in range(2):
                        pool.wait_ge(v_ttr, NCH * QT * b + NCH * (t + 3))
                        load_mask((b + 1) % B, t)
                    pool.wait_ge(v_oA, QT * b + QT)
                    load_x((b + 1) % B)
                root(1)
                for u in range(NCH):
                    split_k(u)
                root(2)
                for u in range(NCH, 2 * NCH):
                    split_k(u)
                with pool.If(b < B - 1):
                    pool.wait_ge(qd_stored, 16 * KD * (b + 1))
                    load_ctx((b + 1) % B)
                    pool.wait_ge(pe_vp, VP * b + VP)
                    pool.nop(nofuse=True)
                    load_ctxT((b + 1) % B)
                root(3)

            pool.wait_ge(pe_oC, QT * B)
            pool.memset(lt, 1.0).then_inc(g_set, 1)
            pool.memset(onesD, 1.0).then_inc(g_set, 1)
            pool.wait_ge(g_set, 10)
            pool.affine_select(out=lt, in_=lt, compare_op=ALU.is_gt, fill=0.0, base=0,
                               pattern=[[1, P]], channel_multiplier=-1).then_inc(g_set, 1)
            for ramp, n in ((iota_e, NE), (iota_k, NE * 2), (iota_t, ET)):
                pool.iota(ramp, pattern=[[1, n]], base=0, channel_multiplier=0,
                          allow_small_or_imprecise_dtypes=True).then_inc(g_set, 1)
            pool.wait_ge(big_loaded, 16)
            pool.wait_ge(v_slot, 1)
            pool.wait_ge(s_zeroed, 16 * (ET * TS // (P * 8)))
            for t in range(NT):
                pool.indirect_dma_start(out=dramS, out_offset=IndirectOffsetOnAxis(ap=slot[:, t:t + 1], axis=0),
                                        in_=big[:, t, :], in_offset=None).then_inc(scattered, 16)
            pool.wait_ge(scattered, 16 * NT)
            for par in range(2):
                pool.wait_ge(ys_stored[par], 16 * (ET // 2))
            for t in range(NT):
                pool.indirect_dma_start(out=big[:, t, :], out_offset=None, in_=dramY,
                                        in_offset=IndirectOffsetOnAxis(ap=slot[:, t:t + 1], axis=0)
                                        ).then_inc(gathered[t // QT], 16)

        @block.scalar
        def _(act):
            act.wait_ge(ld["w"], 16 * NW)
            act.activation(tg[:], tg[:], ACT.Tanh).then_inc(a_set, 1)

            def evac_xT(ln):
                act.wait_ge(pe_xT, 4 * b + ln + 1)
                act.activation(xT[:, 0, :], PS[:, 0, :], ACT.Copy).then_inc(a_xT, 1)

            with act.Fori(0, B) as b:
                evac_xT(0)
                act.wait_ge(pe_qg, 2 * b + 1)
                act.activation(qgA[:, 0, :], PS[:, 2, :], ACT.Copy).then_inc(a_qg, 1)

                def exp_a(t):
                    act.wait_ge(v_nmA, QT * b + t + 1)
                    act.activation(eA[t % 2], eA[t % 2], ACT.Exp, bias=nmA[:, t:t + 1],
                                   accum_out=rsA[:, t:t + 1]).then_inc(a_expA, 1)

                def evac_pa(t):
                    act.wait_ge(pe_ptA, QT * b + t + 1)
                    act.activation(ptA[:, 0:8, t * P:(t + 1) * P],
                                   PS[:, 0:2, :].rearrange("p a (c q) -> p (a c) q", c=4),
                                   ACT.Copy).then_inc(a_ptA, 1)

                exp_a(0)
                exp_a(1)
                evac_pa(0)
                exp_a(2)
                evac_pa(1)
                exp_a(3)
                evac_pa(2)
                evac_pa(3)
                act.wait_ge(pe_otA, 2 * b + 1)
                act.activation(otA[:, 0, :], PS[:, 4, :], ACT.Copy).then_inc(a_otA, 1)

                evac_xT(1)
                act.wait_ge(v_rm, b + 1)
                act.activation(rt[0:1, 2, :], rt[0:1, 1, :], ACT.Exp, accum_out=rt[0:1, 3, 0:1]).then_inc(a_re, 1)

                def high_k(u):
                    n = K_CH[u % NCH][1]
                    act.wait_ge(pe_kp, 8 * b + u + 1)
                    if u >= NCH:
                        act.wait_ge(kd_stored[u % 4], 32 * b + 16)
                    act.activation(kp[u % 4][:, 0, 0:n], PS[:, 4 + u % 4, 0:n], ACT.Identity,
                                   bias=bkC[:, u // NCH:u // NCH + 1]).then_inc(a_kh, 1)

                for u in range(NCH):
                    high_k(u)
                for m in range(2):
                    act.wait_ge(pe_qkvB, 6 * b + 3 + m)
                    act.activation(kB[:, m, :], PS[:, 4 + m, :], ACT.Identity,
                                   bias=bs[:, m, 1:2]).then_inc(a_kB, 1)
                act.wait_ge(pe_qkvB, 6 * b + 5)
                act.activation(vB[:, 0:2, :].rearrange("p t n -> p (t n)"), PS[:, 6, :], ACT.Copy).then_inc(a_vB, 1)

                def evac_pb(i):
                    act.wait_ge(pe_tB, 16 * b + i + 1)
                    if i >= 8:
                        act.wait_ge(pe_pvB, 4 * b + i // 4 - 1)
                    act.activation(ptB[i // 4 % 2][:, :, i % 4 * P:(i % 4 + 1) * P],
                                   PS[:, 4 + i % 2, :].rearrange("p (k q) -> p k q", k=QT),
                                   ACT.Copy).then_inc(a_ptB, 1)

                for i in range(16):
                    act.wait_ge(v_nmB, 16 * b + i + 1)
                    if i >= 4:
                        act.wait_ge(pe_tB, 16 * b + i - 3)
                    act.activation(pB[i % 4], PS[:, i % 4, :], ACT.Exp, bias=nmB[:, i:i + 1],
                                   accum_out=rsB[:, i:i + 1]).then_inc(a_expB, 1)
                    if i >= 2:
                        evac_pb(i - 2)
                evac_pb(14)
                evac_pb(15)

                evac_xT(2)
                act.wait_ge(v_tq, b + 1)
                act.activation(qp[:, 0, :, :], tq, ACT.Copy).then_inc(a_qh, 1)
                for u in range(NCH, 2 * NCH):
                    high_k(u)

                def evac_v(i):
                    act.wait_ge(pe_vp, VP * b + i + 1)
                    bank = 5 + i % 3
                    if 2 * i + 1 < CT:
                        out = vc[:, 2 * i:2 * i + 2, :, 0:DC]
                        src = PS[:, bank, :].rearrange("p (c h d) -> p c h d", c=2, h=HC)
                    else:
                        out = vc[0:CL, 2 * i, :, 0:DC]
                        src = PS[0:CL, bank, 0:D].rearrange("p (h d) -> p h d", h=HC)
                    act.activation(out, src, ACT.Copy).then_inc(a_vp, 1)

                def copy_rows(g):
                    act.wait_ge(pe_mT, NG * b + g + 1)
                    act.activation(mrow[:], PS[0:3 * GH, bank_m(g), 0:S // 2].bitcast(BF16),
                                   ACT.Copy).then_inc(a_mrow, 1)

                for i in range(VP - 1):
                    evac_v(i)
                copy_rows(0)
                evac_v(VP - 1)
                for g in range(NG):
                    for u in range(UN):
                        U = g * UN + u
                        r = rows(u // GH)
                        act.wait_ge(pe_st, NG * UN * b + U + 1)
                        if U >= RING:
                            act.wait_ge(pe_pv, NG * CT * b + (U - RING) // GH + 1)
                        act.activation(pr[U % RING][0:r, :], PS[0:r, 5 + U % 3, :], ACT.Exp).then_inc(a_expC, 1)
                        if u == MT_AT - 1 and g + 1 < NG:
                            copy_rows(g + 1)
                    act.wait_ge(pe_pv, NG * CT * b + CT * (g + 1))
                    act.activation(oc[g % 2], PS[:, 4, :], ACT.Copy).then_inc(a_oc, 1)
                act.wait_ge(pe_aT, 2 * b + 1)
                act.activation(aoT[:, 0, :], PS[:, 0, :], ACT.Copy).then_inc(a_aT, 1)

                evac_xT(3)
                act.wait_ge(v_gd, b + 1)
                act.activation(lgd[:], lgd[:], ACT.Exp).then_inc(a_ge, 1)

            def hidden(j, par, k):
                act.wait_ge(w_loaded[par], 64 * (k + 1))
                for m in range(FM):
                    act.wait_ge(pe_h, 4 * j + m // 2 + 1)
                    act.activation(hT[:, m, :], PS[:, 2 + m // 2, m % 2 * TS:(m % 2 + 1) * TS], ACT.Relu,
                                   bias=b1[par][:, m:m + 1]).then_inc(a_h, 1)

            with act.Fori(0, ET // 2) as jj:
                for par in range(2):
                    hidden(2 * jj + par, par, jj)

        @block.tensor
        def _(pe):
            mm, tr = nc.tensor.matmul, nc.tensor.transpose
            pe.wait_ge(ld["w"], 16 * NW)
            for m in range(KD):
                for k in range(KD):
                    last = mm(PS[:, m, 0:D], qgA[:, k, m * P:(m + 1) * P], qgA[:, k, D:2 * D],
                              start=k == 0, stop=k == KD - 1)
                last.then_inc(pe_set, 1)
            pe.wait_ge(g_set, 7)
            pe.wait_ge(v_set, 6)
            masked = pe.value_load(mflag[0:1, 0:1], min_val=0, max_val=1)

            def transpose_x(ln):
                for t in range(QT):
                    pe.wait_ge(v_xn, 4 * QT * b + QT * ln + t + 1)
                    for k in range(KD):
                        last = tr(PS[:, k, t * P:(t + 1) * P], xn[:, t, k * P:(k + 1) * P], ident[:])
                last.then_inc(pe_xT, 1)

            def wait_xT(ln):
                pe.wait_ge(a_xT, 4 * b + ln + 1)
                pe.wait_ge(v_xT, 4 * b + ln + 1)

            with pe.Fori(0, B) as b:
                transpose_x(0)
                wait_xT(0)
                for m in range(KD):
                    for k in range(KD):
                        last = mm(PS[:, 2 + m, :], gA[:, k, m * P:(m + 1) * P], xT[:, k, :],
                                  start=k == 0, stop=k == KD - 1)
                    last.then_inc(pe_qg, 1)
                pe.wait_ge(a_qg, b + 1)
                pe.wait_ge(v_qg, b + 1)
                pe.wait_ge(ld["ctxT"], 16 * (b + 1))

                def scores_a(t):
                    for i, (c0, n) in enumerate(A_CH):
                        if t:
                            pe.wait_ge(v_ttr, NCH * QT * b + NCH * (t - 1) + i + 1)
                        for k in range(KD):
                            last = mm(PS[:, 4 + i, 0:n], qgA[:, k, t * P:(t + 1) * P], ctxT[:, k, c0:c0 + n],
                                      start=k == 0, stop=k == KD - 1)
                        last.then_inc(pe_sA, 1)

                def transpose_a(t):
                    pe.wait_ge(a_expA, QT * b + t + 1)
                    if t:
                        pe.wait_ge(a_ptA, QT * b + t)
                        pe.wait_ge(v_ptA, QT * b + t)
                    for c in range(CT):
                        last = tr(PS[0:rows(c), c // 4, c % 4 * P:(c % 4 + 1) * P],
                                  eA[t % 2][:, c * P:c * P + rows(c)], ident[:])
                    last.then_inc(pe_ptA, 1)

                scores_a(0)
                scores_a(1)
                transpose_a(0)
                scores_a(2)
                transpose_a(1)
                scores_a(3)
                transpose_a(2)
                transpose_a(3)
                pe.wait_ge(a_ptA, QT * b + QT)
                pe.wait_ge(v_ptA, QT * b + QT)
                pe.wait_ge(ld["ctxN"], 32 * (b + 1))
                for m in range(KD):
                    for c in range(CT):
                        r = rows(c)
                        last = mm(PS[:, 4 + m, :], ctxN[0:r, c, m * P:(m + 1) * P], ptA[0:r, c, :],
                                  start=c == 0, stop=c == CT - 1)
                    last.then_inc(pe_otA, 1)
                pe.wait_ge(a_otA, b + 1)
                pe.wait_ge(v_otA, b + 1)
                for t in range(QT):
                    for k in range(KD):
                        last = mm(PS[:, t, 0:D], otA[:, k, t * P:(t + 1) * P], wvA[:, k, :],
                                  start=k == 0, stop=k == KD - 1)
                    last.then_inc(pe_oA, 1)

                pe.wait_ge(v_oA, QT * b + QT)
                transpose_x(1)
                pe.wait_ge(v_ms, b + 1)
                for k in range(KD):
                    last = mm(PS[0:1, 2, 0:HB], msum[:, k:k + 1], wrB[:, k, :], start=k == 0, stop=k == KD - 1)
                last.then_inc(pe_rl, 1)

                def project_k(u):
                    m, (c0, n) = u // NCH, K_CH[u % NCH]
                    for k in range(KD):
                        last = mm(PS[:, 4 + u % 4, 0:n], wkC[:, k, m * P:(m + 1) * P], ctxT[:, k, c0:c0 + n],
                                  start=k == 0, stop=k == KD - 1)
                    last.then_inc(pe_kp, 1)

                for u in range(NCH):
                    project_k(u)
                pe.wait_ge(ld["ws"], 128 * (b + 1))
                wait_xT(1)
                pe.wait_ge(v_rm, b + 1)
                for m in range(2):
                    for k in range(KD):
                        last = mm(PS[:, 2 + m, :], ws[:, 0, k, 2 * m:2 * m + 2, :], xT[:, k, :],
                                  start=k == 0, stop=k == KD - 1)
                    last.then_inc(pe_qkvB, 1)
                pe.wait_ge(a_kh, 8 * b + NCH)
                pe.wait_ge(v_kr, 8 * b + NCH)
                for m in range(2):
                    for k in range(KD):
                        last = mm(PS[:, 4 + m, :], ws[:, 1, k, 2 * m:2 * m + 2, :], xT[:, k, :],
                                  start=k == 0, stop=k == KD - 1)
                    last.then_inc(pe_qkvB, 1)
                for t in range(QT):
                    for k in range(KD):
                        last = mm(PS[:, 6 + t // 2, t % 2 * D:(t % 2 + 1) * D], xT[:, k, t * P:(t + 1) * P],
                                  ws[:, 2, k, :, :], start=k == 0, stop=k == KD - 1)
                    if t % 2:
                        last.then_inc(pe_qkvB, 1)
                pe.wait_ge(v_qB, 2 * b + 2)
                pe.wait_ge(a_kB, 2 * b + 2)

                def scores_b(i):
                    h, t = i // QT, i % QT
                    q = DB * (h % 2)
                    if i >= 4:
                        pe.wait_ge(a_expB, 16 * b + i - 3)
                    mm(PS[:, i % 4, :], qB[q:q + DB, h // 2, t * P:(t + 1) * P], kB[q:q + DB, h // 2, :],
                       start=True, stop=True).then_inc(pe_sB, 1)

                def transpose_b(i):
                    pe.wait_ge(v_pB, 16 * b + i + 1)
                    if i >= 2:
                        pe.wait_ge(a_ptB, 16 * b + i - 1)
                    for k in range(QT):
                        last = tr(PS[:, 4 + i % 2, k * P:(k + 1) * P], pB[i % 4][:, k * P:(k + 1) * P], ident[:])
                    last.then_inc(pe_tB, 1)

                def values_b(h):
                    q = DB * (h % 2)
                    pe.wait_ge(a_ptB, 16 * b + QT * (h + 1))
                    if h == 0:
                        pe.wait_ge(a_vB, b + 1)
                        pe.wait_ge(v_vB, b + 1)
                    for k in range(QT):
                        last = mm(PS[q:q + DB, 6 + h // 2, :], vB[:, k, h * DB:(h + 1) * DB], ptB[h % 2][:, k, :],
                                  start=k == 0, stop=k == QT - 1)
                    last.then_inc(pe_pvB, 1)

                for i in range(3):
                    scores_b(i)
                for i in range(16):
                    transpose_b(i)
                    if i + 3 < 16:
                        scores_b(i + 3)
                    if i % QT == 1 and i > 1:
                        values_b(i // QT - 1)
                values_b(3)
                pe.wait_ge(v_otB, 2 * b + 2)
                for t in range(QT):
                    for k in range(KD):
                        last = mm(PS[:, t, 0:D], oB[:, k, t * P:(t + 1) * P], woB[:, k, :],
                                  start=k == 0, stop=k == KD - 1)
                    last.then_inc(pe_oB, 1)

                pe.wait_ge(v_oB, QT * b + QT)
                transpose_x(2)
                wait_xT(2)
                for m in range(KD):
                    for k in range(KD):
                        last = mm(PS[:, 2 + m, :], wqC[:, k, m * P:(m + 1) * P], xT[:, k, :],
                                  start=k == 0, stop=k == KD - 1)
                    last.then_inc(pe_qC, 1)
                for u in range(NCH, 2 * NCH):
                    project_k(u)

                def project_v(i):
                    bank = 5 + i % 3
                    if i < 3:
                        pe.wait_ge(a_kh, 8 * b + 6 + min(i, 2))
                        pe.wait_ge(v_kr, 8 * b + 6 + min(i, 2))
                    else:
                        pe.wait_ge(a_vp, VP * b + i - 2)
                    for c in range(2 * i, min(2 * i + 2, CT)):
                        for k in range(KD):
                            last = mm(PS[0:rows(c), bank, c % 2 * D:(c % 2 + 1) * D],
                                      ctxT[:, k, c * P:c * P + rows(c)], wvC[:, k, :],
                                      start=k == 0, stop=k == KD - 1)
                    last.then_inc(pe_vp, 1)

                def scores_c(g, i, with_mask):
                    h, t = i // (QT * 2), i // 2 % QT
                    I = g * NS_C + i
                    if I >= 2:
                        pe.wait_ge(v_mx, NG * NS_C * b + I - 1)
                    elif I == 1:
                        pe.wait_ge(v_tq, b + 1)
                    for j in range(2):
                        c0, n = M_CH[i % 2 * 2 + j]
                        bank = I % 2 * 2 + j
                        last = mm(PS[:, bank, 0:n], qs[g % 3][0:ROWS, h, t * P:(t + 1) * P],
                                  ks[g % 3][0:ROWS, h, c0:c0 + n], start=True, stop=True)
                        if with_mask:
                            for c in range(c0 // P, -(-(c0 + n) // P)):
                                lo, hi = max(c0 - c * P, 0), min(c0 + n - c * P, rows(c))
                                last = mm(PS[:, bank, c * P + lo - c0:c * P + hi - c0],
                                          maskT[0:rows(c), c, t * P:(t + 1) * P], identb[0:rows(c), lo:hi],
                                          start=False, stop=True, skip_group_check=True)
                    last.then_inc(pe_sC, 1)

                def scores_t(g, u, with_mask):
                    c, h = u // GH, u % GH
                    r, U = rows(c), g * UN + u
                    if U >= 3:
                        pe.wait_ge(a_expC, NG * UN * b + U - 2)
                    last = mm(PS[0:r, 5 + U % 3, :], ks[g % 3][0:STK, h, c * P:c * P + r], qs[g % 3][0:STK, h, :],
                              start=True, stop=not with_mask)
                    if with_mask:
                        last = mm(PS[0:r, 5 + U % 3, :], identb[0:r, 0:r], maskT[0:r, c, :],
                                  start=False, stop=True)
                    last.then_inc(pe_st, 1)

                def values_c(g, c):
                    if c == 0 and g:
                        pe.wait_ge(v_ao, NG * b + g)
                    for h in range(GH):
                        U = g * UN + c * GH + h
                        r = rows(c)
                        pe.wait_ge(a_expC, NG * UN * b + U + 1)
                        last = mm(PS[32 * h:32 * h + DC + 1, 4, :], vc[0:r, c, g * GH + h, :],
                                  pr[U % RING][0:r, :], start=c == 0, stop=c == CT - 1)
                    last.then_inc(pe_pv, 1)

                def transpose_m(g):
                    pe.wait_ge(v_np, NG * b + g + 1)
                    if g:
                        pe.wait_ge(a_expC, NG * UN * b + (g - 1) * UN + MT_AT - 2)
                    else:
                        pe.wait_ge(a_vp, VP * b + 5)
                    for t in range(QT):
                        last = tr(PS[0:3 * GH, bank_m(g), t * P // 2:(t + 1) * P // 2].bitcast(BF16),
                                  npt[:, t, :, :].rearrange("p r h -> p (r h)"), identb[:])
                    last.then_inc(pe_mT, 1)

                def transpose_o(g):
                    pe.wait_ge(a_oc, NG * b + g + 1)
                    for t in range(QT):
                        last = tr(PS[:, 4, t * P:(t + 1) * P], oc[g % 2][:, t * P:(t + 1) * P], ident[:])
                    last.then_inc(pe_oT, 1)

                def attention_c(with_mask):
                    done = 0

                    def maxima_to(n):
                        nonlocal done
                        while done < min(n, NG * NS_C):
                            g = done // NS_C
                            if done % NS_C == 0:
                                pe.wait_ge(qs_loaded[g % 3], loads_before(b, g, NR, 0))
                                pe.wait_ge(ks_loaded[g % 3], loads_before(b, g, NR, 1))
                            scores_c(g, done % NS_C, with_mask)
                            done += 1

                    maxima_to(8)
                    project_v(3)
                    maxima_to(18)
                    project_v(4)
                    maxima_to(NS_C)
                    project_v(5)
                    transpose_m(0)
                    project_v(6)
                    maxima_to(NS_C + LEAD)
                    pe.wait_ge(a_vp, VP * b + VP)
                    for g in range(NG):
                        pe.wait_ge(m_loaded, 48 * (NG * b + g + 1))
                        for u in range(UN):
                            if u == MT_AT and g + 1 < NG:
                                transpose_m(g + 1)
                                maxima_to((g + 1) * NS_C + LEAD + (u + 1) * NS_C // UN)
                                pe.wait_ge(a_mrow, NG * b + g + 2)
                            scores_t(g, u, with_mask)
                            maxima_to((g + 1) * NS_C + LEAD + (u + 1) * NS_C // UN)
                            if u % GH == GH - 1 and u > GH:
                                values_c(g, u // GH - 1)
                            if u == 3 and g:
                                transpose_o(g - 1)
                        values_c(g, CT - 1)

                for i in range(3):
                    project_v(i)
                with pe.If(masked != 0):
                    attention_c(True)
                with pe.Else():
                    attention_c(False)
                transpose_o(NG - 1)
                pe.wait_ge(v_ab, b + 1)
                for k in range(KD):
                    for t in range(QT):
                        last = tr(PS[:, k, t * P:(t + 1) * P], ao[:, t, k * P:(k + 1) * P], ident[:])
                    last.then_inc(pe_aT, 1)
                pe.wait_ge(a_aT, b + 1)
                pe.wait_ge(v_aT, b + 1)
                for t in range(QT):
                    for k in range(KD):
                        last = mm(PS[:, 2 + t, 0:D], aoT[:, k, t * P:(t + 1) * P], woC[:, k, :],
                                  start=k == 0, stop=k == KD - 1)
                    last.then_inc(pe_oC, 1)

                transpose_x(3)
                wait_xT(3)
                for t in range(QT):
                    for k in range(KD):
                        last = mm(PS[:, 6, t * NE:(t + 1) * NE], xT[:, k, t * P:(t + 1) * P], wgD[:, k, :],
                                  start=k == 0, stop=k == KD - 1)
                last.then_inc(pe_gate, 1)

            pe.wait_ge(v_oh, 1)
            pe.wait_ge(g_set, 11)
            ohf = oh.rearrange("p t e -> p (t e)")
            mm(PS[:, 0, 0:NT * NE], lt, ohf, start=True, stop=True).then_inc(pe_rank, 1)
            mm(PS[:, 1, 0:NT * NE], onesD, ohf, start=True, stop=True).then_inc(pe_rank, 1)
            pe.wait_ge(v_slot, 1)

            def turn_rows(j, par, k):
                pe.wait_ge(xs_loaded[par], 16 * (k + 1))
                for kk in range(KD):
                    for t in range(2):
                        last = tr(PS[:, par, kk * TS + t * P:kk * TS + (t + 1) * P],
                                  xs[par][:, t, kk * P:(kk + 1) * P], ident[:])
                last.then_inc(pe_xsT, 1)

            def hidden(j, par, k):
                pe.wait_ge(w_loaded[par], 64 * (k + 1))
                pe.wait_ge(v_xsT, j + 1)
                for m in range(FM):
                    for kk in range(KD):
                        last = mm(PS[:, 2 + m // 2, m % 2 * TS:(m % 2 + 1) * TS], w1[par][:, kk, m * P:(m + 1) * P],
                                  xsT[par][:, kk, :], start=kk == 0, stop=kk == KD - 1)
                    if m % 2:
                        last.then_inc(pe_h, 1)

            def outputs(j, par, first=False):
                if not first:
                    pe.wait_ge(v_y, 2 * j)
                for t in range(2):
                    for m in range(FM):
                        pe.wait_ge(a_h, FM * j + m + 1)
                        last = mm(PS[:, 6 + t, 0:D], hT[:, m, t * P:(t + 1) * P], w2[par][:, m, :],
                                  start=m == 0, stop=m == FM - 1)
                    last.then_inc(pe_y, 1)

            def pair(jj, first=False):
                hidden(2 * jj, 0, jj)
                turn_rows(2 * jj + 1, 1, jj)
                outputs(2 * jj, 0, first)
                hidden(2 * jj + 1, 1, jj)
                turn_rows(2 * jj + 2, 0, jj + 1)
                outputs(2 * jj + 1, 1)

            turn_rows(0, 0, 0)
            pair(0, True)
            with pe.Fori(1, ET // 2 - 1) as jj:
                pair(jj)
            hidden(ET - 2, 0, ET // 2 - 1)
            turn_rows(ET - 1, 1, ET // 2 - 1)
            outputs(ET - 2, 0)
            hidden(ET - 1, 1, ET // 2 - 1)
            outputs(ET - 1, 1)

        @block.vector
        def _(dve):
            own = Ticks(v_self)
            v = nc.vector
            v.memset(PS[:, 5:7, :], 0.0).then_inc(v_set, 1)
            v.memset(small[:], 0.0).then_inc(*own.tick())
            mraw = ptA.bitcast(I32)
            dve.wait_ge(ld["mT"], 32)
            v.tensor_scalar(maskT[:, 0:CT - 1, :], mraw[:, 0:CT - 1, :], 0.0, MASKED,
                            ALU.is_equal, ALU.mult).then_inc(*own.tick())
            v.tensor_scalar(maskT[0:CL, CT - 1, :], mraw[0:CL, CT - 1, :], 0.0, MASKED,
                            ALU.is_equal, ALU.mult).then_inc(*own.tick())
            dve.wait_ge(v_self, own.now())
            v.tensor_reduce(small[:, 20:21], maskT[:, 0:CT - 1, :], AX.XY, ALU.min, negate=True).then_inc(*own.tick())
            v.tensor_reduce(small[0:CL, 21:22], maskT[0:CL, CT - 1, :], AX.X, ALU.min,
                            negate=True).then_inc(*own.tick())
            dve.wait_ge(v_self, own.now())
            v.tensor_tensor(small[:, 20:21], small[:, 20:21], small[:, 21:22], ALU.max).then_inc(v_set, 2)
            dve.wait_ge(g_set, 8)
            v.tensor_scalar(mflag[:, 0:1], small[:, 32:33], 0.0, None, ALU.is_gt).then_inc(v_set, 1)
            dve.wait_ge(pe_set, KD)
            v.tensor_scalar(gA[:], PS[:, 0:KD, 0:D], 1.0 / 16.0, None, ALU.mult).then_inc(v_set, 1)
            dve.wait_ge(a_set, 1)
            v.tensor_scalar(boB[:], boB[:], tg[:, 2:3], None, ALU.mult).then_inc(v_set, 1)
            v.tensor_scalar(boC[:], boC[:], tg[:, 1:2], None, ALU.mult).then_inc(*own.tick())
            assert own.n == V_SET, own.n

            def layernorm(ln, src):
                for t in range(QT):
                    v.bn_stats(st[:, t, :], src[:, t, :]).then_inc(*own.tick())
                dve.wait_ge(v_self, own.now())
                dve.nop(nofuse=True)
                for t in range(QT):
                    v.bn_aggr(mv[:, t, :], st[:, t, :]).then_inc(*own.tick())
                dve.wait_ge(v_self, own.now())
                v.tensor_scalar(vpe[:], mv[:, :, 1], EPS, None, ALU.add).then_inc(v_var, 1)
                dve.wait_ge(g_rstd, 4 * b + ln + 1)
                for t in range(QT):
                    v.tensor_scalar(xn[:, t, :], src[:, t, :], mv[:, t, 0:1], rstd[:, t:t + 1],
                                    ALU.subtract, ALU.mult).then_inc(v_xn, 1)

            def evac_xT(ln):
                dve.wait_ge(pe_xT, 4 * b + ln + 1)
                v.tensor_copy(xT[:, 1, :], PS[:, 1, :]).then_inc(v_xT, 1)

            with dve.Fori(0, B) as b:
                own.base, own.n = V_SET + V_PER * b, 0
                dve.wait_ge(ld["x"], 16 * (b + 1))
                layernorm(0, xin)
                evac_xT(0)
                dve.wait_ge(pe_qg, 2 * b + 2)
                v.tensor_copy(qgA[:, 1, :], PS[:, 3, :]).then_inc(v_qg, 1)

                def add_mask(t):
                    dve.wait_ge(ld[f"mk{t % 2}"], 16 * (2 * b + t // 2 + 1))
                    if t >= 2:
                        dve.wait_ge(pe_ptA, QT * b + t - 1)
                    for i, (c0, n) in enumerate(A_CH):
                        dve.wait_ge(pe_sA, QT * NCH * b + NCH * t + i + 1)
                        dve.nop(nofuse=True)
                        v.tensor_tensor_reduce(out=eA[t % 2][:, c0:c0 + n], in0=PS[:, 4 + i, 0:n],
                                               in1=mk[t % 2][:, c0:c0 + n], scale=1.0, scalar=-3.0e38,
                                               op0=ALU.add, op1=ALU.max,
                                               accum_out=mxA[:, i:i + 1]).then_inc(v_ttr, 1)
                    dve.wait_ge(v_ttr, QT * NCH * b + NCH * (t + 1))
                    v.tensor_reduce(nmA[:, t:t + 1], mxA, AX.X, ALU.max, negate=True).then_inc(v_nmA, 1)
                    dve.wait_ge(v_nmA, QT * b + t + 1)

                def evac_pa(t):
                    dve.wait_ge(pe_ptA, QT * b + t + 1)
                    v.tensor_copy(ptA[:, 8:12, t * P:(t + 1) * P],
                                  PS[:, 2, :].rearrange("p (c q) -> p c q", c=4)).then_inc(*own.tick())
                    v.tensor_copy(ptA[0:CL, 12, t * P:(t + 1) * P], PS[0:CL, 3, 0:P]).then_inc(v_ptA, 1)

                add_mask(0)
                add_mask(1)
                evac_pa(0)
                add_mask(2)
                evac_pa(1)
                add_mask(3)
                evac_pa(2)
                evac_pa(3)
                dve.wait_ge(a_expA, QT * b + QT)
                v.reciprocal(rcA, rsA).then_inc(*own.tick())
                dve.wait_ge(v_self, own.now())
                v.tensor_scalar(rcA, rcA, tg[:, 0:1], None, ALU.mult).then_inc(*own.tick())
                dve.wait_ge(pe_otA, 2 * b + 2)
                v.tensor_copy(otA[:, 1, :], PS[:, 5, :]).then_inc(v_otA, 1)
                dve.wait_ge(v_self, own.now())
                for t in range(QT):
                    dve.wait_ge(pe_oA, QT * b + t + 1)
                    v.scalar_tensor_tensor(out=xw[:, t, :], in0=PS[:, t, 0:D], scalar=rcA[:, t:t + 1],
                                           in1=xin[:, t, :], op0=ALU.mult, op1=ALU.add).then_inc(v_oA, 1)
                dve.wait_ge(v_oA, QT * b + QT)

                layernorm(1, xw)
                evac_xT(1)
                dve.wait_ge(v_xT, 4 * b + 2)
                dve.wait_ge(a_xT, 4 * b + 2)
                v.tensor_reduce(msum, xT[:], AX.X, ALU.add).then_inc(v_ms, 1)
                lrow, drow, erow, prow = (rt[0:1, i, :] for i in (0, 1, 2, 4))
                dve.wait_ge(pe_rl, b + 1)
                v.scalar_tensor_tensor(out=lrow, in0=PS[0:1, 2, 0:HB], scalar=1.0 / S, in1=brB[:],
                                       op0=ALU.mult, op1=ALU.add).then_inc(*own.tick())
                dve.wait_ge(v_self, own.now())
                v.tensor_reduce(rt[0:1, 3, 1:2], lrow, AX.X, ALU.max).then_inc(*own.tick())
                dve.wait_ge(v_self, own.now())
                v.tensor_scalar(drow, lrow, rt[0:1, 3, 1:2], None, ALU.subtract).then_inc(v_rm, 1)
                dve.wait_ge(a_re, b + 1)
                v.reciprocal(rt[0:1, 3, 2:3], rt[0:1, 3, 0:1]).then_inc(*own.tick())
                dve.wait_ge(v_self, own.now())
                v.tensor_scalar(prow, erow, rt[0:1, 3, 2:3], None, ALU.mult).then_inc(*own.tick())
                dve.wait_ge(v_self, own.now())
                dve.nop(nofuse=True)
                v.max(rt[0:1, 5, 0:8], prow).then_inc(*own.tick())
                dve.wait_ge(v_self, own.now())
                dve.nop(nofuse=True)
                v.max_index(rti[0:1, 0, :], rt[0:1, 5, 0:8], prow).then_inc(*own.tick())
                v.memset(rt[0:1, 6, 0:8], 0.0).then_inc(*own.tick())
                dve.wait_ge(v_self, own.now())
                v.tensor_scalar(rt[0:1, 6, 0:ACTIVE], rti[0:1, 0, 0:ACTIVE], -1.0, float(HB),
                                ALU.mult, ALU.add).then_inc(*own.tick())
                dve.wait_ge(v_self, own.now())
                dve.nop(nofuse=True)
                v.max(rt[0:1, 7, 0:8], rt[0:1, 6, 0:8]).then_inc(*own.tick())
                dve.wait_ge(v_self, own.now())
                v.tensor_scalar(rti[0:1, 1, :], rt[0:1, 7, 0:8], -1.0, float(HB),
                                ALU.mult, ALU.add).then_inc(v_idx, 1)

                def rest_k(u):
                    m, n = u // NCH, K_CH[u % NCH][1]
                    dve.wait_ge(a_kh, 8 * b + u + 1)
                    if u >= NCH:
                        dve.wait_ge(g_ks, 8 * b + u - 3)
                    v.scalar_tensor_tensor(out=kr[u % 4][:, 0:n], in0=PS[:, 4 + u % 4, 0:n], scalar=bkC[:, m:m + 1],
                                           in1=kp[u % 4][:, 0, 0:n], op0=ALU.add,
                                           op1=ALU.subtract).then_inc(v_kr, 1)

                for u in range(NCH):
                    rest_k(u)
                for m in range(2):
                    dve.wait_ge(pe_qkvB, 6 * b + m + 1)
                    v.tensor_scalar(qB[:, m, :], PS[:, 2 + m, :], bs[:, m, 0:1], 1.0 / 8.0,
                                    ALU.add, ALU.mult).then_inc(v_qB, 1)
                dve.wait_ge(pe_qkvB, 6 * b + 6)
                v.tensor_copy(vB[:, 2:4, :].rearrange("p t n -> p (t n)"), PS[:, 7, :]).then_inc(v_vB, 1)

                def normalise(i):
                    dve.wait_ge(a_expB, 16 * b + i + 1)
                    v.reciprocal(rsB[:, i:i + 1], rsB[:, i:i + 1]).then_inc(*own.tick())
                    dve.wait_ge(v_self, own.now())
                    v.tensor_scalar(pB[i % 4], pB[i % 4], rsB[:, i:i + 1], None, ALU.mult).then_inc(v_pB, 1)

                for i in range(16):
                    dve.wait_ge(pe_sB, 16 * b + i + 1)
                    v.tensor_reduce(nmB[:, i:i + 1], PS[:, i % 4, :], AX.X, ALU.max, negate=True).then_inc(v_nmB, 1)
                    if i:
                        normalise(i - 1)
                normalise(15)
                for m in range(2):
                    dve.wait_ge(pe_pvB, 4 * b + 2 * m + 2)
                    v.tensor_scalar(oB[:, m, :], PS[:, 6 + m, :], bs[:, m, 2:3], None, ALU.add).then_inc(v_otB, 1)

                def residual(pe_out, bank, gate, bias, done):
                    for t in range(QT):
                        dve.wait_ge(pe_out, QT * b + t + 1)
                        v.scalar_tensor_tensor(out=xw[:, t, :], in0=PS[:, bank + t, 0:D], scalar=gate,
                                               in1=xw[:, t, :], op0=ALU.mult, op1=ALU.add).then_inc(*own.tick())
                    for t in range(QT):
                        dve.wait_ge(v_self, own.now())
                        v.tensor_tensor(xw[:, t, :], xw[:, t, :], bias[:], ALU.add).then_inc(done, 1)
                    dve.wait_ge(done, QT * b + QT)

                residual(pe_oB, 0, tg[:, 2:3], boB, v_oB)

                layernorm(2, xw)
                evac_xT(2)
                for m in range(KD):
                    dve.wait_ge(pe_qC, 2 * b + m + 1)
                    ins = v.tensor_scalar(tq[:, m, :], PS[:, 2 + m, :], bqC[:, m:m + 1], 0.25, ALU.add, ALU.mult)
                    ins.then_inc(*own.tick()) if m == 0 else ins.then_inc(v_tq, 1)
                dve.wait_ge(a_qh, b + 1)
                dve.wait_ge(v_self, own.now())
                v.tensor_tensor(tq, tq, qp[:, 0, :, :], ALU.subtract).then_inc(*own.tick())
                dve.wait_ge(v_self, own.now())
                v.tensor_copy(qp[:, 1, :, :], tq).then_inc(*own.tick())
                dve.wait_ge(v_self, own.now())
                v.tensor_tensor(qp[:, 2, :, :], tq, qp[:, 1, :, :], ALU.subtract).then_inc(v_qs, 1)
                for u in range(NCH, 2 * NCH):
                    rest_k(u)

                def maxima(g, i):
                    h, t, I = i // (QT * 2), i // 2 % QT, g * NS_C + i
                    dve.wait_ge(pe_sC, NG * NS_C * b + I + 1)
                    v.tensor_reduce(mxC[:, h, t, i % 2:i % 2 + 1],
                                    PS[:, I % 2 * 2:I % 2 * 2 + 2, 0:M_CH[i % 2 * 2][1]], AX.XY,
                                    ALU.max).then_inc(v_mx, 1)

                def split_m(g):
                    dve.wait_ge(v_mx, NG * NS_C * b + NS_C * (g + 1))
                    v.tensor_reduce(nmC[:].rearrange("p t h -> p h t"), mxC[:], AX.X, ALU.max,
                                    negate=True).then_inc(*own.tick())
                    dve.wait_ge(v_self, own.now())
                    if g:
                        dve.wait_ge(pe_mT, NG * b + g)
                    v.tensor_copy(npt[:, :, 0, :], nmC[:]).then_inc(*own.tick())
                    dve.wait_ge(v_self, own.now())
                    v.tensor_tensor(nmr[:], nmC[:], npt[:, :, 0, :], ALU.subtract).then_inc(*own.tick())
                    dve.wait_ge(v_self, own.now())
                    v.tensor_copy(npt[:, :, 1, :], nmr[:]).then_inc(*own.tick())
                    dve.wait_ge(v_self, own.now())
                    v.tensor_tensor(npt[:, :, 2, :], nmr[:], npt[:, :, 1, :], ALU.subtract).then_inc(v_np, 1)

                def heads_out(g):
                    dve.wait_ge(pe_oT, NG * b + g + 1)
                    src = PS[:, 4, :].rearrange("p (t h d) -> p t h d", t=QT, h=GH)
                    v.reciprocal(rcC[:], src[:, :, :, DC]).then_inc(*own.tick())
                    dve.wait_ge(v_self, own.now())
                    for t in range(QT):
                        ins = v.tensor_tensor(
                            ao[:, t, g * GH * DC:(g + 1) * GH * DC].rearrange("p (h d) -> p h d", h=GH),
                            src[:, t, :, 0:DC], rcC[:, t, :].unsqueeze(2).broadcast_to([P, GH, DC]), ALU.mult)
                        ins.then_inc(*own.tick()) if t < QT - 1 else ins.then_inc(v_ao, 1)

                for g in range(NG):
                    for i in range(NS_C):
                        maxima(g, i)
                        if g >= 2 and i == LEAD + 2:
                            heads_out(g - 2)
                    split_m(g)
                heads_out(NG - 2)
                heads_out(NG - 1)
                dve.wait_ge(v_ao, NG * b + NG)
                v.tensor_tensor(ao[:], ao[:], bvC[:].unsqueeze(1).broadcast_to([P, QT, D]), ALU.add).then_inc(v_ab, 1)
                dve.wait_ge(pe_aT, 2 * b + 2)
                v.tensor_copy(aoT[:, 1, :], PS[:, 1, :]).then_inc(v_aT, 1)
                residual(pe_oC, 2, tg[:, 1:2], boC, v_oC)

                layernorm(3, xw)
                evac_xT(3)
                dve.wait_ge(pe_gate, b + 1)
                v.tensor_tensor(lg[:], PS[:, 6, 0:QT * NE].rearrange("p (t e) -> p t e", t=QT),
                                bgD[:].unsqueeze(1).broadcast_to([P, QT, NE]), ALU.add).then_inc(*own.tick())
                dve.wait_ge(v_self, own.now())
                dve.nop(nofuse=True)
                for t in range(QT):
                    v.max(mx8[:, t, :], lg[:, t, :]).then_inc(*own.tick())
                dve.wait_ge(v_self, own.now())
                v.tensor_tensor(lgd[:], lg[:], mx8[:, :, 0:1].broadcast_to([P, QT, NE]),
                                ALU.subtract).then_inc(v_gd, 1)
                for t in range(QT):
                    v.max_index(ix8[:, t, :], mx8[:, t, :], lg[:, t, :]).then_inc(*own.tick())
                dve.wait_ge(v_self, own.now())
                v.tensor_copy(expert[:, bass.ds(QT * b, QT)], ix8[:, :, 0]).then_inc(*own.tick())
                dve.wait_ge(a_ge, b + 1)
                v.tensor_reduce(ssum[:], lgd[:], AX.X, ALU.add).then_inc(*own.tick())
                dve.wait_ge(v_self, own.now())
                v.reciprocal(weight[:, bass.ds(QT * b, QT)], ssum[:]).then_inc(*own.tick())
                dve.wait_ge(v_self, own.now())
                dve.wait_ge(x_stored, 16 * b + 16)
                dve.wait_ge(n_stored, 16 * b + 16)
                assert own.n == V_PER, own.n

            own.base, own.n = V_SET + V_PER * B, 0

            def alone(ins):
                ins.then_inc(*own.tick())
                dve.wait_ge(v_self, own.now())

            dve.wait_ge(g_set, 14)
            v.tensor_tensor(oh, expert[:].unsqueeze(2).broadcast_to([P, NT, NE]),
                            iota_e.unsqueeze(1).broadcast_to([P, NT, NE]), ALU.is_equal).then_inc(v_oh, 1)
            alone(v.tensor_scalar(weight[:], weight[:], tg[:, 3:4], None, ALU.mult))
            dve.wait_ge(pe_rank, 2)
            alone(v.tensor_copy(tot, PS[:, 1, 0:NT * NE].rearrange("p (t e) -> p t e", t=NT)))
            src, step_ = tot, 1
            n_pass = 0
            while step_ < NT:
                dst = inc[n_pass % 2]
                v.tensor_copy(dst[:, 0:step_, :], src[:, 0:step_, :]).then_inc(*own.tick())
                alone(v.tensor_tensor(dst[:, step_:, :], src[:, step_:, :], src[:, :NT - step_, :], ALU.add))
                src, step_, n_pass = dst, 2 * step_, n_pass + 1
            alone(v.tensor_copy(ncount, src[:, NT - 1, :]))
            alone(v.tensor_tensor(tot, src, tot, ALU.subtract))
            alone(v.tensor_tensor(tot, tot, PS[:, 0, 0:NT * NE].rearrange("p (t e) -> p t e", t=NT), ALU.add))
            alone(v.tensor_scalar(iota_k, iota_k, float(TS), None, ALU.mult))
            alone(v.tensor_tensor(cmp, ncount.unsqueeze(2).broadcast_to([P, NE, NE * 2]),
                                  iota_k.unsqueeze(1).broadcast_to([P, NE, NE * 2]), ALU.is_gt))
            alone(v.tensor_reduce(tiles, cmp, AX.X, ALU.add))
            tsrc, step_, n_pass = tiles, 1, 0
            while step_ < NE:
                dst = tinc[n_pass % 2]
                v.tensor_copy(dst[:, 0:step_], tsrc[:, 0:step_]).then_inc(*own.tick())
                alone(v.tensor_tensor(dst[:, step_:], tsrc[:, step_:], tsrc[:, :NE - step_], ALU.add))
                tsrc, step_, n_pass = dst, 2 * step_, n_pass + 1
            alone(v.tensor_tensor(tbase, tsrc, tiles, ALU.subtract))
            alone(v.tensor_scalar(tbase, tbase, float(TS), None, ALU.mult))
            alone(v.tensor_tensor(tcmp, tsrc.unsqueeze(1).broadcast_to([P, ET, NE]),
                                  iota_t.unsqueeze(2).broadcast_to([P, ET, NE]), ALU.is_le))
            alone(v.tensor_reduce(texf, tcmp, AX.X, ALU.add))
            v.tensor_scalar(tex, texf, float(NE - 1), None, ALU.min).then_inc(v_tex, 1)
            alone(v.tensor_tensor(tot, tot, tbase.unsqueeze(1).broadcast_to([P, NT, NE]), ALU.add))
            alone(v.tensor_tensor(tot, tot, oh, ALU.mult))
            alone(v.tensor_reduce(slotf, tot, AX.X, ALU.add))
            v.tensor_copy(slot, slotf).then_inc(v_slot, 1)

            def rows_in(j, par):
                dve.wait_ge(pe_xsT, j + 1)
                v.tensor_copy(xsT[par].rearrange("p k t -> p (k t)"), PS[:, par, :]).then_inc(v_xsT, 1)

            def rows_out(j, par, k, first=False):
                if not first:
                    dve.wait_ge(ys_stored[par], 16 * k)
                for t in range(2):
                    dve.wait_ge(pe_y, 2 * j + t + 1)
                    v.tensor_tensor(ys[par][:, t, :], PS[:, 6 + t, 0:D], b2[par], ALU.add).then_inc(v_y, 1)

            def pair(jj, first=False):
                rows_in(2 * jj + 1, 1)
                rows_out(2 * jj, 0, jj, first)
                rows_in(2 * jj + 2, 0)
                rows_out(2 * jj + 1, 1, jj, first)

            rows_in(0, 0)
            pair(0, True)
            with dve.Fori(1, ET // 2 - 1) as jj:
                pair(jj)
            rows_in(ET - 1, 1)
            rows_out(ET - 2, 0, ET // 2 - 1)
            rows_out(ET - 1, 1, ET // 2 - 1)
            for t in range(NT):
                bb = t // QT
                dve.wait_ge(gathered[bb], 16 * QT)
                dve.wait_ge(xr_loaded[bb % 2], 16 * (bb // 2 + 1))
                v.scalar_tensor_tensor(out=big[:, t, :], in0=big[:, t, :], scalar=weight[:, t:t + 1],
                                       in1=fin[bb % 2][:, t % QT, :], op0=ALU.mult, op1=ALU.add).then_inc(v_out, 1)


def kernel(**inputs):
    import concourse.bacc as bacc
    from concourse.bass_utils import run_bass_kernel_spmd as run
    import ml_dtypes

    i = {k: np.asarray(v) for k, v in inputs.items()}

    def t(x):
        return np.ascontiguousarray(x.swapaxes(-1, -2))

    qkv = np.stack([i["L0_ffn_Wq"], i["L0_ffn_Wk"], i["L0_ffn_Wv"]])
    arrays = {
        "x": i["x"],
        "ctx": i["ctx_1024"],
        "ctxT": t(i["ctx_1024"]),
        "A_mask": i["mask_BxSxS2_ff0"],
        "C_maskT": t(i["mask_1x1xSxS2_if1"][0, 0]),
        "g_x": i["g_xattn"],
        "g_f": i["g_ffn"],
        "A_WqWk": np.concatenate([i["L0_xattn_W_q"], i["L0_xattn_W_k"]], axis=1),
        "A_WvT": t(i["L0_xattn_W_v"]),
        "B_w": qkv.reshape(3, KD, P, HB, DB).transpose(3, 2, 0, 1, 4),
        "B_b": np.stack([i["L0_ffn_bq"], i["L0_ffn_bk"], i["L0_ffn_bv"]]).reshape(3, HB, DB).transpose(1, 2, 0),
        "B_Wr": i["L0_ffn_Wr"],
        "B_br": i["L0_ffn_br"][None],
        "B_Wo": i["L0_ffn_Wo"],
        "B_bo": i["L0_ffn_bo"],
        "C_WqT": t(i["L1_xattn_w_q"]),
        "C_WkT": t(i["L1_xattn_w_k"]),
        "C_WvT": t(i["L1_xattn_w_v"]),
        "C_WoT": t(i["L1_xattn_w_o"]),
        "C_bq": t(i["L1_xattn_b_q"].reshape(KD, P)),
        "C_bk": t(i["L1_xattn_b_k"].reshape(KD, P)),
        "C_bv": i["L1_xattn_b_v"],
        "C_bo": i["L1_xattn_b_o"],
        "D_wg": i["L1_ffn_w_gate"],
        "D_bg": i["L1_ffn_b_gate"],
        "D_W1": i["L1_ffn_W1"],
        "D_W2": i["L1_ffn_W2"],
        "D_b1": t(i["L1_ffn_b1"].reshape(NE, FM, P)),
        "D_b2": i["L1_ffn_b2"],
        "ones": np.ones((3, GH * C), ml_dtypes.bfloat16),
    }
    nc = bacc.Bacc("TRN2", target_bir_lowering=False, num_devices=1)
    feeds, aps = {}, {}
    for name, x in arrays.items():
        x = np.ascontiguousarray(x)
        feeds[f"in_{name}"] = x
        aps[name] = nc.dram_tensor(f"in_{name}", x.shape, mybir.dt.from_np(x.dtype), kind="ExternalInput").ap()
    aps["out"] = nc.dram_tensor("out", (B, S, D), F32, kind="ExternalOutput").ap()
    flamingo(nc, aps)
    r = run(nc, [feeds], core_ids=[0])
    return r.results[0]["out"]
```

```python
from contextlib import ExitStack

import numpy as np

import concourse.bass as bass
from concourse import mybir
from concourse.bass import IndirectOffsetOnAxis

F32 = mybir.dt.float32
BF16 = mybir.dt.bfloat16
I32 = mybir.dt.int32
U32 = mybir.dt.uint32
ALU = mybir.AluOpType
ACT = mybir.ActivationFunctionType
AX = mybir.AxisListType

B, S, C, D = 8, 512, 1601, 256
P = 128
QT = S // P
KD = D // P
CT = -(-C // P)
CL = C - (CT - 1) * P
EPS = 1e-5
A_CH = [(0, 512), (512, 512), (1024, 512), (1536, C - 1536)]
K_CH = [(0, 384), (384, 384), (768, 384), (1152, C - 1152)]
NCH = 4
M_N = -(-C // NCH)
M_CH = [(0, M_N - 1), (M_N - 1, M_N - 1), (2 * M_N - 2, M_N), (C - M_N, M_N)]
HB, DB, ACTIVE = 16, 64, 4
HC, DC = 16, 16
GH = 4
NG = HC // GH
KPART = (0, 1, 0, 2, 0, 1)
QPART = (0, 0, 1, 0, 2, 1)
NR = len(KPART)
ROWS = NR * DC
STK = ROWS + 3
CMAX = max(n for _, n in K_CH)
NS_C = GH * QT * NCH // 2
LEAD = 8
VP = -(-CT // 2)
UN = CT * GH
MT_AT = UN - 8
RING = 8
NE, FF = 8, 1024
FM = FF // P
TOK = B * S
NT = TOK // P
TS = 256
ET = TOK // TS + NE
MASKED = -float(2.0 ** 100)


class Ticks:

    def __init__(self, sem):
        self.sem, self.base, self.n = sem, 0, 0

    def tick(self):
        self.n += 1
        return self.sem, 1

    def now(self):
        return self.base + self.n


def bank_m(g):
    return 5 + ((g - 1) * UN + MT_AT) % 3 if g else 6


def rows(c):
    return P if c < CT - 1 else CL


def loads_before(b, g, each, ones):
    per_batch = 16 * (each * (2 if g % 3 == 0 else 1) + ones)
    return per_batch * b + 16 * (each * (g // 3 + 1) + ones)


def flamingo(nc, a):
    ctx_stack = ExitStack()
    with ctx_stack:
        def sem(name):
            return ctx_stack.enter_context(nc.semaphore(name))

        def sb(name, shape, dt):
            return ctx_stack.enter_context(nc.sbuf_tensor(name, shape, dt))

        NPS = 8
        PS = ctx_stack.enter_context(nc.psum_tensor("PS", [P, NPS, 512], F32))

        ident = sb("ident", [P, P], F32)
        identb = sb("identb", [P, P], BF16)
        gA = sb("gA", [P, KD, D], F32)
        wvA = sb("wvA", [P, KD, D], F32)
        woB = sb("woB", [P, KD, D], F32)
        wrB = sb("wrB", [P, KD, HB], F32)
        brB = sb("brB", [1, HB], F32)
        wqC = sb("wqC", [P, KD, D], F32)
        wkC = sb("wkC", [P, KD, D], F32)
        wvC = sb("wvC", [P, KD, D], F32)
        woC = sb("woC", [P, KD, D], F32)
        bqC = sb("bqC", [P, KD], F32)
        bkC = sb("bkC", [P, KD], F32)
        bvC = sb("bvC", [P, D], F32)
        boB = sb("boB", [P, D], F32)
        boC = sb("boC", [P, D], F32)
        wgD = sb("wgD", [P, KD, NE], F32)
        bgD = sb("bgD", [P, NE], F32)
        tg = sb("tg", [P, 4], F32)
        mhalf = sb("mhalf", [P, QT], F32)
        maskT = sb("maskT", [P, CT, S], BF16)
        mflag = sb("mflag", [P, 2], I32)
        expert = sb("expert", [P, NT], F32)
        weight = sb("weight", [P, NT], F32)

        xin = sb("xin", [P, QT, D], F32)
        xw = sb("xw", [P, QT, D], F32)
        xn = sb("xn", [P, QT, D], F32)
        xT = sb("xT", [P, KD, S], F32)
        ctxN = sb("ctxN", [P, CT, D], F32)
        ctxT = sb("ctxT", [P, KD, C], F32)
        mk = [sb(f"mk{i}", [P, C], F32) for i in range(2)]
        vc = sb("vc", [P, CT, HC, DC + 1], F32)
        ws = sb("ws", [P, 3, KD, ACTIVE, DB], F32)
        bs = sb("bs", [P, 2, 3], F32)
        st = sb("st", [P, QT, 6], F32)
        mv = sb("mv", [P, QT, 2], F32)
        vpe = sb("vpe", [P, QT], F32)
        rstd = sb("rstd", [P, QT], F32)
        small = sb("small", [P, 64], F32)
        mxA, nmA, rsA, rcA = (small[:, 0:4], small[:, 4:8], small[:, 8:12], small[:, 12:16])
        msum = small[:, 16:18]
        rt = sb("rt", [1, 8, HB], F32)
        rti = sb("rti", [1, 2, 8], U32)
        nmB = sb("nmB", [P, ACTIVE * QT], F32)
        rsB = sb("rsB", [P, ACTIVE * QT], F32)
        mxC = sb("mxC", [P, GH, QT, NCH // 2], F32)
        nmC = sb("nmC", [P, QT, GH], F32)
        nmr = sb("nmr", [P, QT, GH], F32)
        npt = sb("npt", [P, QT, 3, GH], BF16)
        mrow = sb("mrow", [3 * GH, S], BF16)
        rcC = sb("rcC", [P, QT, GH], F32)
        lg = sb("lg", [P, QT, NE], F32)
        lgd = sb("lgd", [P, QT, NE], F32)
        mx8 = sb("mx8", [P, QT, 8], F32)
        ix8 = sb("ix8", [P, QT, 8], U32)
        ssum = sb("ssum", [P, QT], F32)

        def carve(region, size):
            at = [0]

            def take(dims, dt, parts=P):
                n = int(np.prod(dims)) * (4 if dt in (F32, I32, U32) else 2)
                words = -(-n // 4)
                ap = region[0:parts, at[0]:at[0] + words]
                at[0] += words
                assert at[0] <= size, (at[0], size)
                if dt is not F32:
                    ap = ap.bitcast(dt)
                if dt in (BF16,) and words * 2 != int(np.prod(dims)):
                    ap = ap[:, 0:int(np.prod(dims))]
                names = "abcd"[:len(dims)]
                if len(dims) > 1:
                    ap = ap.rearrange(f"p ({' '.join(names)}) -> p {' '.join(names)}",
                                      **{k: v for k, v in zip(names, dims)})
                return ap
            return take

        R1, R2 = 11910, 12700
        reg1 = sb("reg1", [P, R1], F32)
        reg2 = sb("reg2", [P, R2], F32)

        take = carve(reg1, R1)
        ptA = take([CT, S], F32)
        otA = take([KD, S], F32)
        qgA = take([KD, S], F32)
        eA = [take([C], F32) for _ in range(2)]
        take = carve(reg1, R1)
        pr = [take([S], F32) for _ in range(RING)]
        oc = [take([S], F32) for _ in range(2)]
        ao = take([QT, D], F32)
        aoT = take([KD, S], F32)
        kr = [take([CMAX], F32) for _ in range(4)]
        kp = [take([3, CMAX + 1], BF16) for _ in range(4)]
        take = carve(reg2, R2)
        qB = take([2, S], F32)
        kB = take([2, S], F32)
        pB = [take([S], F32) for _ in range(4)]
        ptB = [take([QT, S], F32) for _ in range(2)]
        oB = take([2, S], F32)
        vB = take([QT, ACTIVE * DB], F32)
        take = carve(reg2, R2)
        ks = [take([GH, C], BF16) for _ in range(3)]
        qs = [take([GH, S], BF16) for _ in range(3)]
        tq = ctxN[:, 0:4, :].rearrange("p a b -> p (a b)").rearrange("p (m q) -> p m q", m=KD)
        qp = ctxN[:, 4:10, :].rearrange("p a b -> p (a b)").bitcast(BF16)[:, 0:3 * KD * S].rearrange(
            "p (r m q) -> p r m q", r=3, m=KD)

        take = carve(reg2, R2)
        w1 = [take([KD, FF], F32) for _ in range(2)]
        w2 = [take([FM, D], F32) for _ in range(2)]
        b1 = [take([FM], F32) for _ in range(2)]
        b2 = [take([D], F32) for _ in range(2)]
        xs = [take([2, D], F32) for _ in range(2)]
        xsT = [take([KD, TS], F32) for _ in range(2)]
        take = carve(reg1, R1)
        big = take([NT, D], F32)
        hT = take([FM, TS], F32)
        ys = [take([2, D], F32) for _ in range(2)]
        take = carve(vc[:, :, :, :].rearrange("p a b c -> p (a b c)"), CT * HC * (DC + 1))
        oh = take([NT, NE], F32)
        tot = take([NT, NE], F32)
        inc = [take([NT, NE], F32) for _ in range(2)]
        lt = take([P], F32)
        onesD = take([P], F32)
        ncount = take([NE], F32)
        cmp = take([NE, NE * 2], F32)
        tiles = take([NE], F32)
        tinc = [take([NE], F32) for _ in range(2)]
        tbase = take([NE], F32)
        slotf = take([NT], F32)
        slot = take([NT], I32)
        iota_e = take([NE], F32)
        iota_k = take([NE * 2], F32)
        iota_t = take([ET], F32)
        tcmp = take([ET, NE], F32)
        texf = take([ET], F32)
        tex = take([ET], I32)
        assert NE * 2 == TOK // TS
        fin = [ctxN[:, 0:4, :], ctxN[:, 4:8, :]]

        dramK = nc.dram_tensor("dramK", (3, D, C), BF16, kind="Internal").ap()
        dramQ = nc.dram_tensor("dramQ", (3, D, S), BF16, kind="Internal").ap()
        dramX = nc.dram_tensor("dramX", (B, P, QT, D), F32, kind="Internal").ap()
        dramN = nc.dram_tensor("dramN", (B, P, QT, D), F32, kind="Internal").ap()
        dramS = nc.dram_tensor("dramS", (ET * TS, D), F32, kind="Internal").ap()
        dramY = nc.dram_tensor("dramY", (ET * TS, D), F32, kind="Internal").ap()

        ld = {n: sem("ld_" + n) for n in ("w", "g", "x", "ctxN", "ctxT", "mk0", "mk1", "ws", "mT")}
        kd_stored = [sem(f"kd_stored{i}") for i in range(NCH)]
        qd_stored = sem("qd_stored")
        ks_loaded = [sem(f"ks_loaded{i}") for i in range(3)]
        qs_loaded = [sem(f"qs_loaded{i}") for i in range(3)]
        m_loaded = sem("m_loaded")
        x_stored, n_stored, s_zeroed = sem("x_stored"), sem("n_stored"), sem("s_zeroed")
        N = {}

        def counted(name, per_batch):
            N[name] = per_batch
            return sem(name)

        v_var = counted("v_var", 4)
        g_rstd = counted("g_rstd", 4)
        v_xn = counted("v_xn", 16)
        pe_xT = counted("pe_xT", 4)
        a_xT = counted("a_xT", 4)
        v_xT = counted("v_xT", 4)
        pe_qg = counted("pe_qg", 2)
        v_qg = counted("v_qg", 2)
        pe_sA = counted("pe_sA", 16)
        v_ttr = counted("v_ttr", 16)
        v_nmA = counted("v_nmA", 4)
        a_expA = counted("a_expA", 4)
        pe_ptA = counted("pe_ptA", 4)
        a_ptA = counted("a_ptA", 4)
        v_ptA = counted("v_ptA", 8)
        pe_otA = counted("pe_otA", 2)
        a_otA = counted("a_otA", 1)
        v_otA = counted("v_otA", 1)
        v_rcA = counted("v_rcA", 2)
        pe_oA = counted("pe_oA", 4)
        v_oA = counted("v_oA", 4)
        v_ms = counted("v_ms", 1)
        pe_rl = counted("pe_rl", 1)
        v_rm = counted("v_rm", 1)
        a_re = counted("a_re", 1)
        v_idx = counted("v_idx", 1)
        pe_kp = counted("pe_kp", 8)
        a_kh = counted("a_kh", 8)
        v_kr = counted("v_kr", 8)
        g_ks = counted("g_ks", 8)
        pe_qkvB = counted("pe_qkvB", 6)
        a_kB = counted("a_kB", 2)
        v_qB = counted("v_qB", 2)
        a_vB = counted("a_vB", 1)
        v_vB = counted("v_vB", 1)
        pe_sB = counted("pe_sB", 16)
        v_nmB = counted("v_nmB", 16)
        a_expB = counted("a_expB", 16)
        v_pB = counted("v_pB", 16)
        pe_tB = counted("pe_tB", 16)
        a_ptB = counted("a_ptB", 16)
        pe_pvB = counted("pe_pvB", 4)
        v_otB = counted("v_otB", 2)
        pe_oB = counted("pe_oB", 4)
        v_oB = counted("v_oB", 4)
        pe_qC = counted("pe_qC", 2)
        v_tq = counted("v_tq", 1)
        a_qh = counted("a_qh", 1)
        v_qs = counted("v_qs", 1)
        pe_vp = counted("pe_vp", VP)
        a_vp = counted("a_vp", VP)
        pe_sC = counted("pe_sC", NG * NS_C)
        v_mx = counted("v_mx", NG * NS_C)
        v_np = counted("v_np", NG)
        pe_mT = counted("pe_mT", NG)
        a_mrow = counted("a_mrow", NG)
        pe_st = counted("pe_st", NG * UN)
        a_expC = counted("a_expC", NG * UN)
        pe_pv = counted("pe_pv", NG * CT)
        a_oc = counted("a_oc", NG)
        pe_oT = counted("pe_oT", NG)
        v_ao = counted("v_ao", NG)
        v_ab = counted("v_ab", 2)
        pe_aT = counted("pe_aT", 2)
        a_aT = counted("a_aT", 1)
        v_aT = counted("v_aT", 1)
        pe_oC = counted("pe_oC", 4)
        v_oC = counted("v_oC", 4)
        pe_gate = counted("pe_gate", 1)
        v_lg = counted("v_lg", 1)
        v_gd = counted("v_gd", 1)
        a_ge = counted("a_ge", 1)
        v_self, a_self, g_self = sem("v_self"), sem("a_self"), sem("g_self")
        g_set, v_set, pe_set, a_set = sem("g_set"), sem("v_set"), sem("pe_set"), sem("a_set")
        v_oh, pe_rank, v_slot, v_tex = sem("v_oh"), sem("pe_rank"), sem("v_slot"), sem("v_tex")
        big_loaded, scattered, gathered = sem("big_loaded"), sem("scattered"), [sem(f"gathered{i}") for i in range(B)]
        w_loaded = [sem(f"w_loaded{i}") for i in range(2)]
        xs_loaded = [sem(f"xs_loaded{i}") for i in range(2)]
        pe_xsT, v_xsT, pe_h, a_h, pe_y, v_y = (sem(n) for n in ("pe_xsT", "v_xsT", "pe_h", "a_h", "pe_y", "v_y"))
        ys_stored = [sem(f"ys_stored{i}") for i in range(2)]
        xr_loaded = [sem(f"xr_loaded{i}") for i in range(2)]
        v_out, out_stored = sem("v_out"), sem("out_stored")

        V_SET, V_PER = 14, 105
        NW = 18

        block = ctx_stack.enter_context(nc.Block())

        @block.sync
        def _(sp):
            k2 = "(k p) n -> p k n"
            for dst, src in (
                    (wvA[:], a["A_WvT"].rearrange(k2, p=P)), (woB[:], a["B_Wo"].rearrange(k2, p=P)),
                    (wrB[:], a["B_Wr"].rearrange(k2, p=P)), (brB[:], a["B_br"]),
                    (wqC[:], a["C_WqT"].rearrange(k2, p=P)), (wkC[:], a["C_WkT"].rearrange(k2, p=P)),
                    (wvC[:], a["C_WvT"].rearrange(k2, p=P)), (woC[:], a["C_WoT"].rearrange(k2, p=P)),
                    (bqC[:], a["C_bq"]), (bkC[:], a["C_bk"]),
                    (bvC[:], a["C_bv"].partition_broadcast(P)), (boB[:], a["B_bo"].partition_broadcast(P)),
                    (boC[:], a["C_bo"].partition_broadcast(P)),
                    (wgD[:], a["D_wg"].rearrange(k2, p=P)), (bgD[:], a["D_bg"].partition_broadcast(P)),
                    (tg[:, 0:2], a["g_x"].partition_broadcast(P)),
                    (tg[:, 2:4], a["g_f"].partition_broadcast(P)),
                    (qgA, a["A_WqWk"].rearrange(k2, p=P))):
                sp.dma_start(dst, src).then_inc(ld["w"], 16)
            mraw = ptA.bitcast(I32)
            sp.dma_start(mraw[:, 0:CT - 1, :],
                         a["C_maskT"][0:(CT - 1) * P, :].rearrange("(c p) q -> p c q", p=P)).then_inc(ld["mT"], 16)
            sp.dma_start(mraw[0:CL, CT - 1, :], a["C_maskT"][(CT - 1) * P:C, :]).then_inc(ld["mT"], 16)
            sp.wait_ge(g_set, 4)
            for i in range(ET * TS // (P * 8)):
                sp.dma_start(dramS[i * P * 8:(i + 1) * P * 8, :].rearrange("(p r) n -> p r n", p=P),
                             reg2[:, 0:8 * D].rearrange("p (r n) -> p r n", r=8)).then_inc(s_zeroed, 16)
            sp.wait_ge(s_zeroed, 16 * (ET * TS // (P * 8)))

            with sp.Fori(0, B) as b:
                sp.wait_ge(v_idx, b + 1)
                sp.nop(nofuse=True)
                for j in range(ACTIVE):
                    h = sp.value_load(rti[0:1, 1, j:j + 1], min_val=0, max_val=HB - 1)
                    sp.dma_start(ws[:, :, :, j, :], a["B_w"][bass.ds(h, 1)].rearrange("o p m k n -> (o p) m k n")
                                 ).then_inc(ld["ws"], 16)
                    q = DB * (j % 2)
                    sp.dma_start(bs[q:q + DB, j // 2, :],
                                 a["B_b"][bass.ds(h, 1)].rearrange("o p m -> (o p) m")).then_inc(ld["ws"], 16)

                def store_k(u):
                    m, (c0, n) = u // NCH, K_CH[u % NCH]
                    sp.wait_ge(g_ks, 8 * b + u + 1)
                    sp.dma_start(dramK[:, m * P:(m + 1) * P, c0:c0 + n].rearrange("r p c -> p r c"),
                                 kp[u % 4][:, :, 0:n]).then_inc(kd_stored[u % 4], 16)

                def load_k(g):
                    for r, part in enumerate(KPART):
                        sp.dma_start(ks[g % 3][r * DC:(r + 1) * DC, :, :],
                                     dramK[part, g * GH * DC:(g + 1) * GH * DC, :].rearrange(
                                         "(h d) c -> d h c", d=DC)).then_inc(ks_loaded[g % 3], 16)

                def load_q(g):
                    for r, part in enumerate(QPART):
                        sp.dma_start(qs[g % 3][r * DC:(r + 1) * DC, :, :],
                                     dramQ[part, g * GH * DC:(g + 1) * GH * DC, :].rearrange(
                                         "(h d) q -> d h q", d=DC)).then_inc(qs_loaded[g % 3], 16)

                for u in range(NCH):
                    store_k(u)
                sp.wait_ge(v_oB, QT * b + QT)
                for i in range(3):
                    sp.dma_start(ks[i][ROWS:STK, :, :], a["ones"].rearrange("r (h c) -> r h c", h=GH)
                                 ).then_inc(ks_loaded[i], 16)
                for i in range(NCH):
                    sp.wait_ge(kd_stored[i], 32 * b + 16)
                load_k(0)
                load_k(1)
                sp.wait_ge(v_qs, b + 1)
                for m in range(KD):
                    sp.dma_start(dramQ[:, m * P:(m + 1) * P, :].rearrange("r p q -> p r q"),
                                 qp[:, :, m, :]).then_inc(qd_stored, 16)
                sp.wait_ge(qd_stored, 16 * KD * (b + 1))
                for g in range(3):
                    load_q(g)
                for u in range(NCH, 2 * NCH):
                    store_k(u)
                for i in range(NCH):
                    sp.wait_ge(kd_stored[i], 32 * b + 32)
                load_k(2)
                for g in range(NG):
                    sp.wait_ge(a_mrow, NG * b + g + 1)
                    for r in range(3):
                        sp.dma_start(qs[g % 3][ROWS + r:ROWS + r + 1, :, :],
                                     mrow[r * GH:(r + 1) * GH, :]).then_inc(m_loaded, 16)
                    if g == 1:
                        sp.wait_ge(pe_pv, CT * NG * b + CT)
                        load_q(3)
                        load_k(3)
                sp.wait_ge(v_oC, QT * b + QT)
                sp.dma_start(dramX[bass.ds(b, 1)].rearrange("o p t n -> (o p) t n"), xw[:]).then_inc(x_stored, 16)
                sp.wait_ge(v_xn, QT * (4 * b + 5))
                sp.dma_start(dramN[bass.ds(b, 1)].rearrange("o p t n -> (o p) t n"), xn[:]).then_inc(n_stored, 16)

            sp.wait_ge(n_stored, 16 * B)
            sp.wait_ge(x_stored, 16 * B)
            sp.wait_ge(v_gd, B)
            sp.wait_ge(a_expA, QT * B + 2)
            sp.dma_start(big.rearrange("p (b t) n -> p b t n", b=B), dramN.rearrange("b p t n -> p b t n")
                         ).then_inc(big_loaded, 16)
            sp.wait_ge(v_tex, 1)

            def load_weights(j, par):
                e = sp.value_load(tex[0:1, bass.ds(j, 1)], min_val=0, max_val=NE - 1)
                sp.dma_start(w1[par], a["D_W1"][bass.ds(e, 1)].rearrange("o (k p) f -> p (o k) f", p=P)
                             ).then_inc(w_loaded[par], 16)
                sp.dma_start(w2[par], a["D_W2"][bass.ds(e, 1)].rearrange("o (k p) n -> p (o k) n", p=P)
                             ).then_inc(w_loaded[par], 16)
                sp.dma_start(b1[par], a["D_b1"][bass.ds(e, 1)].rearrange("o p m -> (o p) m")
                             ).then_inc(w_loaded[par], 16)
                sp.dma_start(b2[par], a["D_b2"][bass.ds(e, 1)].rearrange("o n -> (o n)").partition_broadcast(P)
                             ).then_inc(w_loaded[par], 16)

            def load_rows(j, par):
                sp.dma_start(xs[par], dramS[bass.ds(TS * j, TS), :].rearrange("(t p) n -> p t n", p=P)
                             ).then_inc(xs_loaded[par], 16)

            def store_rows(j, par):
                sp.wait_ge(v_y, 2 * j + 2)
                sp.dma_start(dramY[bass.ds(TS * j, TS), :].rearrange("(t p) n -> p t n", p=P),
                             ys[par]).then_inc(ys_stored[par], 16)

            load_weights(0, 0)
            load_weights(1, 1)
            sp.wait_ge(scattered, 16 * NT)
            load_rows(0, 0)
            load_rows(1, 1)
            with sp.Fori(0, ET // 2 - 1) as jj:
                for par in range(2):
                    store_rows(2 * jj + par, par)
                    load_rows(2 * jj + par + 2, par)
                    load_weights(2 * jj + par + 2, par)
            for par in range(2):
                store_rows(ET - 2 + par, par)
            for b in range(B + 1):
                if b >= 1:
                    sp.wait_ge(v_out, QT * b)
                    sp.dma_start(a["out"][b - 1].rearrange("(t p) n -> p t n", p=P),
                                 big[:, QT * (b - 1):QT * b, :]).then_inc(out_stored, 16)
                if b < B:
                    sp.dma_start(fin[b % 2], dramX[b]).then_inc(xr_loaded[b % 2], 16)
            sp.wait_ge(out_stored, 16 * B)

        @block.gpsimd
        def _(pool):
            pool.memset(ident[:], 0.0).then_inc(g_set, 1)
            pool.memset(identb[:], 0.0).then_inc(g_set, 1)
            pool.memset(reg2[:, 0:8 * D], 0.0).then_inc(g_set, 1)
            pool.memset(mhalf[:], -0.5).then_inc(g_set, 1)
            pool.wait_ge(g_set, 4)
            for m in (ident, identb):
                pool.affine_select(out=m[:], in_=m[:], compare_op=ALU.not_equal, fill=1.0, base=0,
                                   pattern=[[-1, P]], channel_multiplier=1).then_inc(g_set, 1)
            pool.memset(vc[:, :, :, DC:DC + 1], 1.0).then_inc(g_set, 1)
            pool.wait_ge(v_set, 3)
            pool.partition_all_reduce(small[:, 32:33], small[:, 20:21], P,
                                      bass.bass_isa.ReduceOp.max).then_inc(g_set, 1)

            def load_x(b):
                pool.dma_start(xin[:], a["x"][bass.ds(b, 1)].rearrange("o (t p) n -> p (o t) n", p=P)
                               ).then_inc(ld["x"], 16)

            def load_ctx(b):
                src = a["ctx"][bass.ds(b, 1)].rearrange("o c n -> (o c) n")
                pool.dma_start(ctxN[:, 0:CT - 1, :], src[0:(CT - 1) * P, :].rearrange("(c p) n -> p c n", p=P)
                               ).then_inc(ld["ctxN"], 16)
                pool.dma_start(ctxN[0:CL, CT - 1, :], src[(CT - 1) * P:C, :]).then_inc(ld["ctxN"], 16)

            def load_ctxT(b):
                pool.dma_start(ctxT[:], a["ctxT"][bass.ds(b, 1)].rearrange("o (k p) c -> p (o k) c", p=P)
                               ).then_inc(ld["ctxT"], 16)

            def load_mask(b, t):
                src = a["A_mask"][bass.ds(b, 1)].rearrange("o q c -> (o q) c")
                pool.dma_start(mk[t % 2][:], src[t * P:(t + 1) * P, :]).then_inc(ld[f"mk{t % 2}"], 16)

            load_x(0)
            load_ctxT(0)
            load_mask(0, 0)
            load_mask(0, 1)
            load_ctx(0)

            def root(n):
                pool.wait_ge(v_var, n + 1)
                pool.tensor_tensor(rstd[:], vpe[:], mhalf[:], ALU.pow).then_inc(g_rstd, 1)

            def split_k(u):
                n = K_CH[u % NCH][1]
                pool.wait_ge(v_kr, 8 * b + u + 1)
                pool.nop(nofuse=True)
                pool.tensor_copy(kp[u % 4][:, 1, 0:n], kr[u % 4][:, 0:n]).then_inc(g_self, 1)
                pool.wait_ge(g_self, 8 * b + u + 1)
                pool.tensor_tensor(kp[u % 4][:, 2, 0:n], kr[u % 4][:, 0:n], kp[u % 4][:, 1, 0:n],
                                   ALU.subtract).then_inc(g_ks, 1)

            def late_masks(bb, src):
                for t in range(2, QT):
                    pool.wait_ge(v_ttr, NCH * QT * bb + NCH * (t - 1))
                    load_mask(src, t)

            root(0)
            late_masks(0, 0)
            with pool.Fori(0, B) as b:
                for t in range(2):
                    pool.wait_ge(v_ttr, NCH * QT * b + NCH * (t + 3))
                    load_mask((b + 1) % B, t)
                pool.wait_ge(v_oA, QT * b + QT)
                load_x((b + 1) % B)
                root(4 * b + 1)
                for u in range(NCH):
                    split_k(u)
                root(4 * b + 2)
                for u in range(NCH, 2 * NCH):
                    split_k(u)
                with pool.If(b < B - 1):
                    pool.wait_ge(qd_stored, 16 * KD * (b + 1))
                    load_ctx((b + 1) % B)
                pool.wait_ge(pe_vp, VP * b + VP)
                pool.nop(nofuse=True)
                load_ctxT((b + 1) % B)
                root(4 * b + 3)
                with pool.If(b < B - 1):
                    late_masks(b + 1, (b + 1) % B)
                root(4 * b + 4)

            pool.wait_ge(pe_oC, QT * B)
            pool.memset(lt, 1.0).then_inc(g_set, 1)
            pool.memset(onesD, 1.0).then_inc(g_set, 1)
            pool.wait_ge(g_set, 10)
            pool.affine_select(out=lt, in_=lt, compare_op=ALU.is_gt, fill=0.0, base=0,
                               pattern=[[1, P]], channel_multiplier=-1).then_inc(g_set, 1)
            for ramp, n in ((iota_e, NE), (iota_k, NE * 2), (iota_t, ET)):
                pool.iota(ramp, pattern=[[1, n]], base=0, channel_multiplier=0,
                          allow_small_or_imprecise_dtypes=True).then_inc(g_set, 1)
            pool.wait_ge(big_loaded, 16)
            pool.wait_ge(v_slot, 1)
            pool.wait_ge(s_zeroed, 16 * (ET * TS // (P * 8)))
            for t in range(NT):
                pool.indirect_dma_start(out=dramS, out_offset=IndirectOffsetOnAxis(ap=slot[:, t:t + 1], axis=0),
                                        in_=big[:, t, :], in_offset=None).then_inc(scattered, 16)
            pool.wait_ge(scattered, 16 * NT)
            for par in range(2):
                pool.wait_ge(ys_stored[par], 16 * (ET // 2))
            for t in range(NT):
                pool.indirect_dma_start(out=big[:, t, :], out_offset=None, in_=dramY,
                                        in_offset=IndirectOffsetOnAxis(ap=slot[:, t:t + 1], axis=0)
                                        ).then_inc(gathered[t // QT], 16)

        @block.scalar
        def _(act):
            act.wait_ge(ld["w"], 16 * NW)
            act.activation(tg[:], tg[:], ACT.Tanh).then_inc(a_set, 1)

            def evac_xT(n):
                act.wait_ge(pe_xT, n + 1)
                act.activation(xT[:, 0, :], PS[:, 0, :], ACT.Copy).then_inc(a_xT, 1)

            def exp_a(bb, t):
                act.wait_ge(v_nmA, QT * bb + t + 1)
                act.activation(eA[t % 2], eA[t % 2], ACT.Exp, bias=nmA[:, t:t + 1],
                               accum_out=rsA[:, t:t + 1]).then_inc(a_expA, 1)

            def evac_pa(bb, t):
                act.wait_ge(pe_ptA, QT * bb + t + 1)
                act.activation(ptA[:, 0:8, t * P:(t + 1) * P],
                               PS[:, 0:2, :].rearrange("p a (c q) -> p (a c) q", c=4),
                               ACT.Copy).then_inc(a_ptA, 1)

            def rest_a(bb):
                evac_pa(bb, 0)
                exp_a(bb, 2)
                evac_pa(bb, 1)
                exp_a(bb, 3)
                evac_pa(bb, 2)
                evac_pa(bb, 3)
                act.wait_ge(pe_otA, 2 * bb + 1)
                act.activation(otA[:, 0, :], PS[:, 4, :], ACT.Copy).then_inc(a_otA, 1)

            exp_a(0, 0)
            exp_a(0, 1)
            rest_a(0)
            with act.Fori(0, B) as b:
                evac_xT(4 * b + 1)
                act.wait_ge(v_rm, b + 1)
                act.activation(rt[0:1, 2, :], rt[0:1, 1, :], ACT.Exp, accum_out=rt[0:1, 3, 0:1]).then_inc(a_re, 1)

                def high_k(u):
                    n = K_CH[u % NCH][1]
                    act.wait_ge(pe_kp, 8 * b + u + 1)
                    if u >= NCH:
                        act.wait_ge(kd_stored[u % 4], 32 * b + 16)
                    act.activation(kp[u % 4][:, 0, 0:n], PS[:, 4 + u % 4, 0:n], ACT.Identity,
                                   bias=bkC[:, u // NCH:u // NCH + 1]).then_inc(a_kh, 1)

                for u in range(NCH):
                    high_k(u)
                for m in range(2):
                    act.wait_ge(pe_qkvB, 6 * b + 3 + m)
                    act.activation(kB[:, m, :], PS[:, 4 + m, :], ACT.Identity,
                                   bias=bs[:, m, 1:2]).then_inc(a_kB, 1)
                act.wait_ge(pe_qkvB, 6 * b + 5)
                act.activation(vB[:, 0:2, :].rearrange("p t n -> p (t n)"), PS[:, 6, :], ACT.Copy).then_inc(a_vB, 1)

                def evac_pb(i):
                    act.wait_ge(pe_tB, 16 * b + i + 1)
                    if i >= 8:
                        act.wait_ge(pe_pvB, 4 * b + i // 4 - 1)
                    act.activation(ptB[i // 4 % 2][:, :, i % 4 * P:(i % 4 + 1) * P],
                                   PS[:, 4 + i % 2, :].rearrange("p (k q) -> p k q", k=QT),
                                   ACT.Copy).then_inc(a_ptB, 1)

                for i in range(16):
                    act.wait_ge(v_nmB, 16 * b + i + 1)
                    if i >= 4:
                        act.wait_ge(pe_tB, 16 * b + i - 3)
                    act.activation(pB[i % 4], PS[:, i % 4, :], ACT.Exp, bias=nmB[:, i:i + 1],
                                   accum_out=rsB[:, i:i + 1]).then_inc(a_expB, 1)
                    if i >= 2:
                        evac_pb(i - 2)
                evac_pb(14)
                evac_pb(15)

                evac_xT(4 * b + 2)
                act.wait_ge(v_tq, b + 1)
                act.activation(qp[:, 0, :, :], tq, ACT.Copy).then_inc(a_qh, 1)
                for u in range(NCH, 2 * NCH):
                    high_k(u)

                def evac_v(i):
                    act.wait_ge(pe_vp, VP * b + i + 1)
                    bank = 5 + i % 3
                    if 2 * i + 1 < CT:
                        out = vc[:, 2 * i:2 * i + 2, :, 0:DC]
                        src = PS[:, bank, :].rearrange("p (c h d) -> p c h d", c=2, h=HC)
                    else:
                        out = vc[0:CL, 2 * i, :, 0:DC]
                        src = PS[0:CL, bank, 0:D].rearrange("p (h d) -> p h d", h=HC)
                    act.activation(out, src, ACT.Copy).then_inc(a_vp, 1)

                def copy_rows(g):
                    act.wait_ge(pe_mT, NG * b + g + 1)
                    act.activation(mrow[:], PS[0:3 * GH, bank_m(g), 0:S // 2].bitcast(BF16),
                                   ACT.Copy).then_inc(a_mrow, 1)

                for i in range(VP - 1):
                    evac_v(i)
                copy_rows(0)
                evac_v(VP - 1)
                for g in range(NG):
                    for u in range(UN):
                        U = g * UN + u
                        r = rows(u // GH)
                        act.wait_ge(pe_st, NG * UN * b + U + 1)
                        if U >= RING:
                            act.wait_ge(pe_pv, NG * CT * b + (U - RING) // GH + 1)
                        act.activation(pr[U % RING][0:r, :], PS[0:r, 5 + U % 3, :], ACT.Exp).then_inc(a_expC, 1)
                        if u == MT_AT - 1 and g + 1 < NG:
                            copy_rows(g + 1)
                    act.wait_ge(pe_pv, NG * CT * b + CT * (g + 1))
                    act.activation(oc[g % 2], PS[:, 4, :], ACT.Copy).then_inc(a_oc, 1)
                exp_a(b + 1, 0)
                act.wait_ge(pe_aT, 2 * b + 1)
                act.activation(aoT[:, 0, :], PS[:, 6, :], ACT.Copy).then_inc(a_aT, 1)
                exp_a(b + 1, 1)
                with act.If(b < B - 1):
                    rest_a(b + 1)
                act.wait_ge(v_gd, b + 1)
                act.activation(lgd[:], lgd[:], ACT.Exp).then_inc(a_ge, 1)

            def hidden(j, par, k):
                act.wait_ge(w_loaded[par], 64 * (k + 1))
                for m in range(FM):
                    act.wait_ge(pe_h, 4 * j + m // 2 + 1)
                    act.activation(hT[:, m, :], PS[:, 2 + m // 2, m % 2 * TS:(m % 2 + 1) * TS], ACT.Relu,
                                   bias=b1[par][:, m:m + 1]).then_inc(a_h, 1)

            with act.Fori(0, ET // 2) as jj:
                for par in range(2):
                    hidden(2 * jj + par, par, jj)

        @block.tensor
        def _(pe):
            mm, tr = nc.tensor.matmul, nc.tensor.transpose
            pe.wait_ge(ld["w"], 16 * NW)
            for m in range(KD):
                for k in range(KD):
                    last = mm(PS[:, m, 0:D], qgA[:, k, m * P:(m + 1) * P], qgA[:, k, D:2 * D],
                              start=k == 0, stop=k == KD - 1)
                last.then_inc(pe_set, 1)
            pe.wait_ge(g_set, 7)
            pe.wait_ge(v_set, 6)
            masked = pe.value_load(mflag[0:1, 0:1], min_val=0, max_val=1)

            def transpose_x(n):
                for t in range(QT):
                    pe.wait_ge(v_xn, QT * n + t + 1)
                    for k in range(KD):
                        last = tr(PS[:, k, t * P:(t + 1) * P], xn[:, t, k * P:(k + 1) * P], ident[:])
                last.then_inc(pe_xT, 1)

            def project_qg(bb, m):
                for k in range(KD):
                    last = mm(PS[:, 2 + m, :], gA[:, k, m * P:(m + 1) * P], xT[:, k, :],
                              start=k == 0, stop=k == KD - 1)
                last.then_inc(pe_qg, 1)

            def score_a(bb, t, i):
                c0, n = A_CH[i]
                if t % 2:
                    pe.wait_ge(v_ttr, NCH * QT * bb + NCH * (t - 1) + i + 1)
                for k in range(KD):
                    last = mm(PS[:, t // 2 * 4 + i, 0:n], qgA[:, k, t * P:(t + 1) * P], ctxT[:, k, c0:c0 + n],
                              start=k == 0, stop=k == KD - 1)
                last.then_inc(pe_sA, 1)

            def transpose_a(bb, t):
                pe.wait_ge(a_expA, QT * bb + t + 1)
                if t:
                    pe.wait_ge(a_ptA, QT * bb + t)
                    pe.wait_ge(v_ptA, 2 * (QT * bb + t))
                else:
                    pe.wait_ge(v_ttr, NCH * QT * bb + 2 * NCH)
                for c in range(CT):
                    last = tr(PS[0:rows(c), c // 4, c % 4 * P:(c % 4 + 1) * P],
                              eA[t % 2][:, c * P:c * P + rows(c)], ident[:])
                last.then_inc(pe_ptA, 1)

            def rest_a(bb):
                transpose_a(bb, 1)
                for i in range(NCH):
                    score_a(bb, 3, i)
                transpose_a(bb, 2)
                transpose_a(bb, 3)
                pe.wait_ge(a_ptA, QT * bb + QT)
                pe.wait_ge(v_ptA, 2 * (QT * bb + QT))
                pe.wait_ge(ld["ctxN"], 32 * (bb + 1))
                for m in range(KD):
                    for c in range(CT):
                        r = rows(c)
                        last = mm(PS[:, 4 + m, :], ctxN[0:r, c, m * P:(m + 1) * P], ptA[0:r, c, :],
                                  start=c == 0, stop=c == CT - 1)
                    last.then_inc(pe_otA, 1)
                pe.wait_ge(a_otA, bb + 1)
                pe.wait_ge(v_otA, bb + 1)
                for t in range(QT):
                    for k in range(KD):
                        last = mm(PS[:, t, 0:D], otA[:, k, t * P:(t + 1) * P], wvA[:, k, :],
                                  start=k == 0, stop=k == KD - 1)
                    last.then_inc(pe_oA, 1)

            transpose_x(0)
            pe.wait_ge(v_xT, 2)
            for m in range(KD):
                project_qg(0, m)
            pe.wait_ge(v_qg, 2)
            pe.wait_ge(ld["ctxT"], 16)
            for t in range(2):
                for i in range(NCH):
                    score_a(0, t, i)
            transpose_a(0, 0)
            for i in range(NCH):
                score_a(0, 2, i)
            rest_a(0)

            with pe.Fori(0, B) as b:
                pe.wait_ge(v_oA, QT * b + QT)
                transpose_x(4 * b + 1)
                pe.wait_ge(v_ms, b + 1)
                for k in range(KD):
                    last = mm(PS[0:1, 2, 0:HB], msum[:, k:k + 1], wrB[:, k, :], start=k == 0, stop=k == KD - 1)
                last.then_inc(pe_rl, 1)

                def project_k(u):
                    m, (c0, n) = u // NCH, K_CH[u % NCH]
                    for k in range(KD):
                        last = mm(PS[:, 4 + u % 4, 0:n], wkC[:, k, m * P:(m + 1) * P], ctxT[:, k, c0:c0 + n],
                                  start=k == 0, stop=k == KD - 1)
                    last.then_inc(pe_kp, 1)

                for u in range(NCH):
                    project_k(u)
                pe.wait_ge(ld["ws"], 128 * (b + 1))
                pe.wait_ge(a_xT, 2 * b + 1)
                pe.wait_ge(v_xT, 6 * b + 3)
                pe.wait_ge(v_rm, b + 1)
                for m in range(2):
                    for k in range(KD):
                        last = mm(PS[:, 2 + m, :], ws[:, 0, k, 2 * m:2 * m + 2, :], xT[:, k, :],
                                  start=k == 0, stop=k == KD - 1)
                    last.then_inc(pe_qkvB, 1)
                pe.wait_ge(a_kh, 8 * b + NCH)
                pe.wait_ge(v_kr, 8 * b + NCH)
                for m in range(2):
                    for k in range(KD):
                        last = mm(PS[:, 4 + m, :], ws[:, 1, k, 2 * m:2 * m + 2, :], xT[:, k, :],
                                  start=k == 0, stop=k == KD - 1)
                    last.then_inc(pe_qkvB, 1)
                for t in range(QT):
                    for k in range(KD):
                        last = mm(PS[:, 6 + t // 2, t % 2 * D:(t % 2 + 1) * D], xT[:, k, t * P:(t + 1) * P],
                                  ws[:, 2, k, :, :], start=k == 0, stop=k == KD - 1)
                    if t % 2:
                        last.then_inc(pe_qkvB, 1)
                pe.wait_ge(v_qB, 2 * b + 2)
                pe.wait_ge(a_kB, 2 * b + 2)

                def scores_b(i):
                    h, t = i // QT, i % QT
                    q = DB * (h % 2)
                    if i >= 4:
                        pe.wait_ge(a_expB, 16 * b + i - 3)
                    mm(PS[:, i % 4, :], qB[q:q + DB, h // 2, t * P:(t + 1) * P], kB[q:q + DB, h // 2, :],
                       start=True, stop=True).then_inc(pe_sB, 1)

                def transpose_b(i):
                    pe.wait_ge(v_pB, 16 * b + i + 1)
                    if i >= 2:
                        pe.wait_ge(a_ptB, 16 * b + i - 1)
                    for k in range(QT):
                        last = tr(PS[:, 4 + i % 2, k * P:(k + 1) * P], pB[i % 4][:, k * P:(k + 1) * P], ident[:])
                    last.then_inc(pe_tB, 1)

                def values_b(h):
                    q = DB * (h % 2)
                    pe.wait_ge(a_ptB, 16 * b + QT * (h + 1))
                    if h == 0:
                        pe.wait_ge(a_vB, b + 1)
                        pe.wait_ge(v_vB, b + 1)
                    for k in range(QT):
                        last = mm(PS[q:q + DB, 6 + h // 2, :], vB[:, k, h * DB:(h + 1) * DB], ptB[h % 2][:, k, :],
                                  start=k == 0, stop=k == QT - 1)
                    last.then_inc(pe_pvB, 1)

                for i in range(3):
                    scores_b(i)
                for i in range(16):
                    transpose_b(i)
                    if i + 3 < 16:
                        scores_b(i + 3)
                    if i % QT == 1 and i > 1:
                        values_b(i // QT - 1)
                values_b(3)
                pe.wait_ge(v_otB, 2 * b + 2)
                for t in range(QT):
                    for k in range(KD):
                        last = mm(PS[:, t, 0:D], oB[:, k, t * P:(t + 1) * P], woB[:, k, :],
                                  start=k == 0, stop=k == KD - 1)
                    last.then_inc(pe_oB, 1)

                pe.wait_ge(v_oB, QT * b + QT)
                transpose_x(4 * b + 2)
                pe.wait_ge(a_xT, 2 * b + 2)
                pe.wait_ge(v_xT, 6 * b + 4)
                for m in range(KD):
                    for k in range(KD):
                        last = mm(PS[:, 2 + m, :], wqC[:, k, m * P:(m + 1) * P], xT[:, k, :],
                                  start=k == 0, stop=k == KD - 1)
                    last.then_inc(pe_qC, 1)
                for u in range(NCH, 2 * NCH):
                    project_k(u)

                def project_v(i):
                    bank = 5 + i % 3
                    if i < 3:
                        pe.wait_ge(a_kh, 8 * b + 6 + min(i, 2))
                        pe.wait_ge(v_kr, 8 * b + 6 + min(i, 2))
                    else:
                        pe.wait_ge(a_vp, VP * b + i - 2)
                    for c in range(2 * i, min(2 * i + 2, CT)):
                        for k in range(KD):
                            last = mm(PS[0:rows(c), bank, c % 2 * D:(c % 2 + 1) * D],
                                      ctxT[:, k, c * P:c * P + rows(c)], wvC[:, k, :],
                                      start=k == 0, stop=k == KD - 1)
                    last.then_inc(pe_vp, 1)

                def scores_c(g, i, with_mask):
                    h, t = i // (QT * 2), i // 2 % QT
                    I = g * NS_C + i
                    if I >= 2:
                        pe.wait_ge(v_mx, NG * NS_C * b + I - 1)
                    elif I == 1:
                        pe.wait_ge(v_tq, b + 1)
                    for j in range(2):
                        c0, n = M_CH[i % 2 * 2 + j]
                        bank = I % 2 * 2 + j
                        last = mm(PS[:, bank, 0:n], qs[g % 3][0:ROWS, h, t * P:(t + 1) * P],
                                  ks[g % 3][0:ROWS, h, c0:c0 + n], start=True, stop=True)
                        if with_mask:
                            for c in range(c0 // P, -(-(c0 + n) // P)):
                                lo, hi = max(c0 - c * P, 0), min(c0 + n - c * P, rows(c))
                                last = mm(PS[:, bank, c * P + lo - c0:c * P + hi - c0],
                                          maskT[0:rows(c), c, t * P:(t + 1) * P], identb[0:rows(c), lo:hi],
                                          start=False, stop=True, skip_group_check=True)
                    last.then_inc(pe_sC, 1)

                def scores_t(g, u, with_mask):
                    c, h = u // GH, u % GH
                    r, U = rows(c), g * UN + u
                    if U >= 3:
                        pe.wait_ge(a_expC, NG * UN * b + U - 2)
                    last = mm(PS[0:r, 5 + U % 3, :], ks[g % 3][0:STK, h, c * P:c * P + r], qs[g % 3][0:STK, h, :],
                              start=True, stop=not with_mask)
                    if with_mask:
                        last = mm(PS[0:r, 5 + U % 3, :], identb[0:r, 0:r], maskT[0:r, c, :],
                                  start=False, stop=True)
                    last.then_inc(pe_st, 1)

                def values_c(g, c):
                    if c == 0 and g:
                        pe.wait_ge(v_ao, NG * b + g)
                    for h in range(GH):
                        U = g * UN + c * GH + h
                        r = rows(c)
                        pe.wait_ge(a_expC, NG * UN * b + U + 1)
                        last = mm(PS[32 * h:32 * h + DC + 1, 4, :], vc[0:r, c, g * GH + h, :],
                                  pr[U % RING][0:r, :], start=c == 0, stop=c == CT - 1)
                    last.then_inc(pe_pv, 1)

                def transpose_m(g):
                    pe.wait_ge(v_np, NG * b + g + 1)
                    if g:
                        pe.wait_ge(a_expC, NG * UN * b + (g - 1) * UN + MT_AT - 2)
                    else:
                        pe.wait_ge(a_vp, VP * b + 5)
                    for t in range(QT):
                        last = tr(PS[0:3 * GH, bank_m(g), t * P // 2:(t + 1) * P // 2].bitcast(BF16),
                                  npt[:, t, :, :].rearrange("p r h -> p (r h)"), identb[:])
                    last.then_inc(pe_mT, 1)

                def transpose_o(g):
                    pe.wait_ge(a_oc, NG * b + g + 1)
                    for t in range(QT):
                        last = tr(PS[:, 4, t * P:(t + 1) * P], oc[g % 2][:, t * P:(t + 1) * P], ident[:])
                    last.then_inc(pe_oT, 1)

                def head_a(u):
                    if u == 2:
                        pe.wait_ge(v_mx, NG * NS_C * (b + 1))
                        transpose_x(4 * b + 3)
                    if u in (8, 12):
                        if u == 8:
                            pe.wait_ge(v_xT, 6 * b + 6)
                        project_qg(b + 1, (u - 8) // 4)
                    if u >= 18 and u % 4 == 2:
                        i = (u - 18) // 4
                        if i == 0:
                            pe.wait_ge(v_qg, 2 * b + 4)
                            pe.wait_ge(ld["ctxT"], 16 * (b + 2))
                        if i < 2 * NCH:
                            score_a(b + 1, i // NCH, i % NCH)

                def attention_c(with_mask):
                    done = 0

                    def maxima_to(n):
                        nonlocal done
                        while done < min(n, NG * NS_C):
                            g = done // NS_C
                            if done % NS_C == 0:
                                pe.wait_ge(qs_loaded[g % 3], loads_before(b, g, NR, 0))
                                pe.wait_ge(ks_loaded[g % 3], loads_before(b, g, NR, 1))
                            scores_c(g, done % NS_C, with_mask)
                            done += 1

                    maxima_to(8)
                    project_v(3)
                    maxima_to(18)
                    project_v(4)
                    maxima_to(NS_C)
                    project_v(5)
                    transpose_m(0)
                    project_v(6)
                    maxima_to(NS_C + LEAD)
                    pe.wait_ge(a_vp, VP * b + VP)
                    for g in range(NG):
                        pe.wait_ge(m_loaded, 48 * (NG * b + g + 1))
                        for u in range(UN):
                            if u == MT_AT and g + 1 < NG:
                                transpose_m(g + 1)
                                maxima_to((g + 1) * NS_C + LEAD + (u + 1) * NS_C // UN)
                                pe.wait_ge(a_mrow, NG * b + g + 2)
                            scores_t(g, u, with_mask)
                            maxima_to((g + 1) * NS_C + LEAD + (u + 1) * NS_C // UN)
                            if u % GH == GH - 1 and u > GH:
                                values_c(g, u // GH - 1)
                            if u == 3 and g:
                                transpose_o(g - 1)
                            if g == NG - 1:
                                head_a(u)
                        values_c(g, CT - 1)

                for i in range(3):
                    project_v(i)
                with pe.If(masked != 0):
                    attention_c(True)
                with pe.Else():
                    attention_c(False)
                transpose_o(NG - 1)
                pe.wait_ge(v_ab, 2 * b + 2)
                for k in range(KD):
                    for t in range(QT):
                        last = tr(PS[:, 6 + k, t * P:(t + 1) * P], ao[:, t, k * P:(k + 1) * P], ident[:])
                    last.then_inc(pe_aT, 1)
                pe.wait_ge(a_aT, b + 1)
                pe.wait_ge(v_aT, b + 1)
                for t in range(QT):
                    for k in range(KD):
                        last = mm(PS[:, 4 + t, 0:D], aoT[:, k, t * P:(t + 1) * P], woC[:, k, :],
                                  start=k == 0, stop=k == KD - 1)
                    last.then_inc(pe_oC, 1)

                with pe.If(b < B - 1):
                    transpose_a(b + 1, 0)
                    for i in range(NCH):
                        pe.wait_ge(v_oC, QT * b + i + 1)
                        score_a(b + 1, 2, i)
                    pe.wait_ge(a_ptA, QT * (b + 1) + 1)
                    pe.wait_ge(v_ptA, 2 * (QT * (b + 1) + 1))
                pe.wait_ge(v_ttr, NCH * QT * (b + 1) + 2 * NCH)
                transpose_x(4 * b + 4)
                pe.wait_ge(v_xT, 6 * b + 8)
                for t in range(QT):
                    for k in range(KD):
                        last = mm(PS[:, 2, t * NE:(t + 1) * NE], xT[:, k, t * P:(t + 1) * P], wgD[:, k, :],
                                  start=k == 0, stop=k == KD - 1)
                last.then_inc(pe_gate, 1)
                with pe.If(b < B - 1):
                    pe.wait_ge(v_lg, b + 1)
                    rest_a(b + 1)

            pe.wait_ge(v_oh, 1)
            pe.wait_ge(g_set, 11)
            ohf = oh.rearrange("p t e -> p (t e)")
            mm(PS[:, 0, 0:NT * NE], lt, ohf, start=True, stop=True).then_inc(pe_rank, 1)
            mm(PS[:, 1, 0:NT * NE], onesD, ohf, start=True, stop=True).then_inc(pe_rank, 1)
            pe.wait_ge(v_slot, 1)

            def turn_rows(j, par, k):
                pe.wait_ge(xs_loaded[par], 16 * (k + 1))
                for kk in range(KD):
                    for t in range(2):
                        last = tr(PS[:, par, kk * TS + t * P:kk * TS + (t + 1) * P],
                                  xs[par][:, t, kk * P:(kk + 1) * P], ident[:])
                last.then_inc(pe_xsT, 1)

            def hidden(j, par, k):
                pe.wait_ge(w_loaded[par], 64 * (k + 1))
                pe.wait_ge(v_xsT, j + 1)
                for m in range(FM):
                    for kk in range(KD):
                        last = mm(PS[:, 2 + m // 2, m % 2 * TS:(m % 2 + 1) * TS], w1[par][:, kk, m * P:(m + 1) * P],
                                  xsT[par][:, kk, :], start=kk == 0, stop=kk == KD - 1)
                    if m % 2:
                        last.then_inc(pe_h, 1)

            def outputs(j, par, first=False):
                if not first:
                    pe.wait_ge(v_y, 2 * j)
                for t in range(2):
                    for m in range(FM):
                        pe.wait_ge(a_h, FM * j + m + 1)
                        last = mm(PS[:, 6 + t, 0:D], hT[:, m, t * P:(t + 1) * P], w2[par][:, m, :],
                                  start=m == 0, stop=m == FM - 1)
                    last.then_inc(pe_y, 1)

            def pair(jj, first=False):
                hidden(2 * jj, 0, jj)
                turn_rows(2 * jj + 1, 1, jj)
                outputs(2 * jj, 0, first)
                hidden(2 * jj + 1, 1, jj)
                turn_rows(2 * jj + 2, 0, jj + 1)
                outputs(2 * jj + 1, 1)

            turn_rows(0, 0, 0)
            pair(0, True)
            with pe.Fori(1, ET // 2 - 1) as jj:
                pair(jj)
            hidden(ET - 2, 0, ET // 2 - 1)
            turn_rows(ET - 1, 1, ET // 2 - 1)
            outputs(ET - 2, 0)
            hidden(ET - 1, 1, ET // 2 - 1)
            outputs(ET - 1, 1)

        @block.vector
        def _(dve):
            own = Ticks(v_self)
            v = nc.vector
            v.memset(PS[:, 5:7, :], 0.0).then_inc(v_set, 1)
            v.memset(small[:], 0.0).then_inc(*own.tick())
            mraw = ptA.bitcast(I32)
            dve.wait_ge(ld["mT"], 32)
            v.tensor_scalar(maskT[:, 0:CT - 1, :], mraw[:, 0:CT - 1, :], 0.0, MASKED,
                            ALU.is_equal, ALU.mult).then_inc(*own.tick())
            v.tensor_scalar(maskT[0:CL, CT - 1, :], mraw[0:CL, CT - 1, :], 0.0, MASKED,
                            ALU.is_equal, ALU.mult).then_inc(*own.tick())
            dve.wait_ge(v_self, own.now())
            v.tensor_reduce(small[:, 20:21], maskT[:, 0:CT - 1, :], AX.XY, ALU.min, negate=True).then_inc(*own.tick())
            v.tensor_reduce(small[0:CL, 21:22], maskT[0:CL, CT - 1, :], AX.X, ALU.min,
                            negate=True).then_inc(*own.tick())
            dve.wait_ge(v_self, own.now())
            v.tensor_tensor(small[:, 20:21], small[:, 20:21], small[:, 21:22], ALU.max).then_inc(v_set, 2)
            dve.wait_ge(g_set, 8)
            v.tensor_scalar(mflag[:, 0:1], small[:, 32:33], 0.0, None, ALU.is_gt).then_inc(v_set, 1)
            dve.wait_ge(pe_set, KD)
            v.tensor_scalar(gA[:], PS[:, 0:KD, 0:D], 1.0 / 16.0, None, ALU.mult).then_inc(v_set, 1)
            dve.wait_ge(a_set, 1)
            v.tensor_scalar(boB[:], boB[:], tg[:, 2:3], None, ALU.mult).then_inc(v_set, 1)
            v.tensor_scalar(boC[:], boC[:], tg[:, 1:2], None, ALU.mult).then_inc(*own.tick())

            def layernorm(n, src):
                for t in range(QT):
                    v.bn_stats(st[:, t, :], src[:, t, :]).then_inc(*own.tick())
                dve.wait_ge(v_self, own.now())
                dve.nop(nofuse=True)
                for t in range(QT):
                    v.bn_aggr(mv[:, t, :], st[:, t, :]).then_inc(*own.tick())
                dve.wait_ge(v_self, own.now())
                v.tensor_scalar(vpe[:], mv[:, :, 1], EPS, None, ALU.add).then_inc(v_var, 1)
                dve.wait_ge(g_rstd, n + 1)
                for t in range(QT):
                    v.tensor_scalar(xn[:, t, :], src[:, t, :], mv[:, t, 0:1], rstd[:, t:t + 1],
                                    ALU.subtract, ALU.mult).then_inc(v_xn, 1)

            def evac_xT(n, both=False):
                dve.wait_ge(pe_xT, n + 1)
                if both:
                    v.tensor_copy(xT[:, 0, :], PS[:, 0, :]).then_inc(v_xT, 1)
                v.tensor_copy(xT[:, 1, :], PS[:, 1, :]).then_inc(v_xT, 1)

            def evac_qg(bb):
                for m in range(KD):
                    dve.wait_ge(pe_qg, 2 * bb + m + 1)
                    v.tensor_copy(qgA[:, m, :], PS[:, 2 + m, :]).then_inc(v_qg, 1)

            def add_mask(bb, t):
                dve.wait_ge(ld[f"mk{t % 2}"], 16 * (2 * bb + t // 2 + 1))
                if t:
                    dve.wait_ge(v_nmA, QT * bb + t)
                if t >= 2:
                    dve.wait_ge(pe_ptA, QT * bb + t - 1)
                for i, (c0, n) in enumerate(A_CH):
                    dve.wait_ge(pe_sA, QT * NCH * bb + NCH * t + i + 1)
                    dve.nop(nofuse=True)
                    v.tensor_tensor_reduce(out=eA[t % 2][:, c0:c0 + n], in0=PS[:, t // 2 * 4 + i, 0:n],
                                           in1=mk[t % 2][:, c0:c0 + n], scale=1.0, scalar=-3.0e38,
                                           op0=ALU.add, op1=ALU.max,
                                           accum_out=mxA[:, i:i + 1]).then_inc(v_ttr, 1)
                dve.wait_ge(v_ttr, QT * NCH * bb + NCH * (t + 1))
                v.tensor_reduce(nmA[:, t:t + 1], mxA, AX.X, ALU.max, negate=True).then_inc(v_nmA, 1)

            def evac_pa(bb, t):
                dve.wait_ge(pe_ptA, QT * bb + t + 1)
                v.tensor_copy(ptA[:, 8:12, t * P:(t + 1) * P],
                              PS[:, 2, :].rearrange("p (c q) -> p c q", c=4)).then_inc(v_ptA, 1)
                v.tensor_copy(ptA[0:CL, 12, t * P:(t + 1) * P], PS[0:CL, 3, 0:P]).then_inc(v_ptA, 1)

            def rest_a(bb, stored=None):
                evac_pa(bb, 1)
                add_mask(bb, 3)
                evac_pa(bb, 2)
                evac_pa(bb, 3)
                dve.wait_ge(a_expA, QT * bb + QT)
                v.reciprocal(rcA, rsA).then_inc(v_rcA, 1)
                dve.wait_ge(v_rcA, 2 * bb + 1)
                v.tensor_scalar(rcA, rcA, tg[:, 0:1], None, ALU.mult).then_inc(v_rcA, 1)
                dve.wait_ge(pe_otA, 2 * bb + 2)
                v.tensor_copy(otA[:, 1, :], PS[:, 5, :]).then_inc(v_otA, 1)
                dve.wait_ge(v_rcA, 2 * bb + 2)
                if stored is not None:
                    dve.wait_ge(x_stored, stored)
                for t in range(QT):
                    dve.wait_ge(pe_oA, QT * bb + t + 1)
                    v.scalar_tensor_tensor(out=xw[:, t, :], in0=PS[:, t, 0:D], scalar=rcA[:, t:t + 1],
                                           in1=xin[:, t, :], op0=ALU.mult, op1=ALU.add).then_inc(v_oA, 1)

            dve.wait_ge(ld["x"], 16)
            layernorm(0, xin)
            evac_xT(0, both=True)
            evac_qg(0)
            add_mask(0, 0)
            add_mask(0, 1)
            evac_pa(0, 0)
            add_mask(0, 2)
            rest_a(0)
            assert own.n == V_SET, own.n
            with dve.Fori(0, B) as b:
                own.base, own.n = V_SET + V_PER * b, 0
                dve.wait_ge(v_oA, QT * b + QT)
                layernorm(4 * b + 1, xw)
                evac_xT(4 * b + 1)
                dve.wait_ge(v_xT, 6 * b + 3)
                dve.wait_ge(a_xT, 2 * b + 1)
                v.tensor_reduce(msum, xT[:], AX.X, ALU.add).then_inc(v_ms, 1)
                lrow, drow, erow, prow = (rt[0:1, i, :] for i in (0, 1, 2, 4))
                dve.wait_ge(pe_rl, b + 1)
                v.scalar_tensor_tensor(out=lrow, in0=PS[0:1, 2, 0:HB], scalar=1.0 / S, in1=brB[:],
                                       op0=ALU.mult, op1=ALU.add).then_inc(*own.tick())
                dve.wait_ge(v_self, own.now())
                v.tensor_reduce(rt[0:1, 3, 1:2], lrow, AX.X, ALU.max).then_inc(*own.tick())
                dve.wait_ge(v_self, own.now())
                v.tensor_scalar(drow, lrow, rt[0:1, 3, 1:2], None, ALU.subtract).then_inc(v_rm, 1)
                dve.wait_ge(a_re, b + 1)
                v.reciprocal(rt[0:1, 3, 2:3], rt[0:1, 3, 0:1]).then_inc(*own.tick())
                dve.wait_ge(v_self, own.now())
                v.tensor_scalar(prow, erow, rt[0:1, 3, 2:3], None, ALU.mult).then_inc(*own.tick())
                dve.wait_ge(v_self, own.now())
                dve.nop(nofuse=True)
                v.max(rt[0:1, 5, 0:8], prow).then_inc(*own.tick())
                dve.wait_ge(v_self, own.now())
                dve.nop(nofuse=True)
                v.max_index(rti[0:1, 0, :], rt[0:1, 5, 0:8], prow).then_inc(*own.tick())
                v.memset(rt[0:1, 6, 0:8], 0.0).then_inc(*own.tick())
                dve.wait_ge(v_self, own.now())
                v.tensor_scalar(rt[0:1, 6, 0:ACTIVE], rti[0:1, 0, 0:ACTIVE], -1.0, float(HB),
                                ALU.mult, ALU.add).then_inc(*own.tick())
                dve.wait_ge(v_self, own.now())
                dve.nop(nofuse=True)
                v.max(rt[0:1, 7, 0:8], rt[0:1, 6, 0:8]).then_inc(*own.tick())
                dve.wait_ge(v_self, own.now())
                v.tensor_scalar(rti[0:1, 1, :], rt[0:1, 7, 0:8], -1.0, float(HB),
                                ALU.mult, ALU.add).then_inc(v_idx, 1)

                def rest_k(u):
                    m, n = u // NCH, K_CH[u % NCH][1]
                    dve.wait_ge(a_kh, 8 * b + u + 1)
                    if u >= NCH:
                        dve.wait_ge(g_ks, 8 * b + u - 3)
                    v.scalar_tensor_tensor(out=kr[u % 4][:, 0:n], in0=PS[:, 4 + u % 4, 0:n], scalar=bkC[:, m:m + 1],
                                           in1=kp[u % 4][:, 0, 0:n], op0=ALU.add,
                                           op1=ALU.subtract).then_inc(v_kr, 1)

                v.tensor_tensor(xw[:], xw[:], boB[:].unsqueeze(1).broadcast_to([P, QT, D]),
                                ALU.add).then_inc(*own.tick())
                for u in range(NCH):
                    rest_k(u)
                for m in range(2):
                    dve.wait_ge(pe_qkvB, 6 * b + m + 1)
                    v.tensor_scalar(qB[:, m, :], PS[:, 2 + m, :], bs[:, m, 0:1], 1.0 / 8.0,
                                    ALU.add, ALU.mult).then_inc(v_qB, 1)
                dve.wait_ge(pe_qkvB, 6 * b + 6)
                v.tensor_copy(vB[:, 2:4, :].rearrange("p t n -> p (t n)"), PS[:, 7, :]).then_inc(v_vB, 1)

                def normalise(i):
                    dve.wait_ge(a_expB, 16 * b + i + 1)
                    v.reciprocal(rsB[:, i:i + 1], rsB[:, i:i + 1]).then_inc(*own.tick())
                    dve.wait_ge(v_self, own.now())
                    v.tensor_scalar(pB[i % 4], pB[i % 4], rsB[:, i:i + 1], None, ALU.mult).then_inc(v_pB, 1)

                for i in range(16):
                    dve.wait_ge(pe_sB, 16 * b + i + 1)
                    v.tensor_reduce(nmB[:, i:i + 1], PS[:, i % 4, :], AX.X, ALU.max, negate=True).then_inc(v_nmB, 1)
                    if i:
                        normalise(i - 1)
                normalise(15)
                for m in range(2):
                    dve.wait_ge(pe_pvB, 4 * b + 2 * m + 2)
                    v.tensor_scalar(oB[:, m, :], PS[:, 6 + m, :], bs[:, m, 2:3], None, ALU.add).then_inc(v_otB, 1)

                def residual(pe_out, bank, gate, done):
                    dve.wait_ge(v_self, own.now())
                    for t in range(QT):
                        dve.wait_ge(pe_out, QT * b + t + 1)
                        v.scalar_tensor_tensor(out=xw[:, t, :], in0=PS[:, bank + t, 0:D], scalar=gate,
                                               in1=xw[:, t, :], op0=ALU.mult, op1=ALU.add).then_inc(done, 1)
                    dve.wait_ge(done, QT * b + QT)

                residual(pe_oB, 0, tg[:, 2:3], v_oB)

                layernorm(4 * b + 2, xw)
                evac_xT(4 * b + 2)
                for m in range(KD):
                    dve.wait_ge(pe_qC, 2 * b + m + 1)
                    ins = v.tensor_scalar(tq[:, m, :], PS[:, 2 + m, :], bqC[:, m:m + 1], 0.25, ALU.add, ALU.mult)
                    ins.then_inc(*own.tick()) if m == 0 else ins.then_inc(v_tq, 1)
                dve.wait_ge(a_qh, b + 1)
                dve.wait_ge(v_self, own.now())
                v.tensor_tensor(tq, tq, qp[:, 0, :, :], ALU.subtract).then_inc(*own.tick())
                dve.wait_ge(v_self, own.now())
                v.tensor_copy(qp[:, 1, :, :], tq).then_inc(*own.tick())
                dve.wait_ge(v_self, own.now())
                v.tensor_tensor(qp[:, 2, :, :], tq, qp[:, 1, :, :], ALU.subtract).then_inc(v_qs, 1)
                for u in range(NCH, 2 * NCH):
                    rest_k(u)
                v.tensor_tensor(xw[:], xw[:], boC[:].unsqueeze(1).broadcast_to([P, QT, D]),
                                ALU.add).then_inc(*own.tick())

                def maxima(g, i):
                    h, t, I = i // (QT * 2), i // 2 % QT, g * NS_C + i
                    dve.wait_ge(pe_sC, NG * NS_C * b + I + 1)
                    v.tensor_reduce(mxC[:, h, t, i % 2:i % 2 + 1],
                                    PS[:, I % 2 * 2:I % 2 * 2 + 2, 0:M_CH[i % 2 * 2][1]], AX.XY,
                                    ALU.max).then_inc(v_mx, 1)

                def split_m(g):
                    dve.wait_ge(v_mx, NG * NS_C * b + NS_C * (g + 1))
                    v.tensor_reduce(nmC[:].rearrange("p t h -> p h t"), mxC[:], AX.X, ALU.max,
                                    negate=True).then_inc(*own.tick())
                    dve.wait_ge(v_self, own.now())
                    if g:
                        dve.wait_ge(pe_mT, NG * b + g)
                    v.tensor_copy(npt[:, :, 0, :], nmC[:]).then_inc(*own.tick())
                    dve.wait_ge(v_self, own.now())
                    v.tensor_tensor(nmr[:], nmC[:], npt[:, :, 0, :], ALU.subtract).then_inc(*own.tick())
                    dve.wait_ge(v_self, own.now())
                    v.tensor_copy(npt[:, :, 1, :], nmr[:]).then_inc(*own.tick())
                    dve.wait_ge(v_self, own.now())
                    v.tensor_tensor(npt[:, :, 2, :], nmr[:], npt[:, :, 1, :], ALU.subtract).then_inc(v_np, 1)

                def heads_out(g):
                    dve.wait_ge(pe_oT, NG * b + g + 1)
                    src = PS[:, 4, :].rearrange("p (t h d) -> p t h d", t=QT, h=GH)
                    v.reciprocal(rcC[:], src[:, :, :, DC]).then_inc(*own.tick())
                    dve.wait_ge(v_self, own.now())
                    for t in range(QT):
                        ins = v.tensor_tensor(
                            ao[:, t, g * GH * DC:(g + 1) * GH * DC].rearrange("p (h d) -> p h d", h=GH),
                            src[:, t, :, 0:DC], rcC[:, t, :].unsqueeze(2).broadcast_to([P, GH, DC]), ALU.mult)
                        ins.then_inc(*own.tick()) if t < QT - 1 else ins.then_inc(v_ao, 1)

                for g in range(NG):
                    for i in range(NS_C):
                        maxima(g, i)
                        if g >= 2 and i == LEAD + 2:
                            heads_out(g - 2)
                    split_m(g)
                dve.wait_ge(ld["x"], 16 * (b + 2))
                layernorm(4 * b + 3, xin)
                heads_out(NG - 2)
                evac_xT(4 * b + 3, both=True)
                evac_qg(b + 1)
                add_mask(b + 1, 0)
                add_mask(b + 1, 1)
                def values_bias(lo, hi):
                    v.tensor_tensor(ao[:, :, lo:hi], ao[:, :, lo:hi],
                                    bvC[:, lo:hi].unsqueeze(1).broadcast_to([P, QT, hi - lo]),
                                    ALU.add).then_inc(v_ab, 1)

                dve.wait_ge(v_ao, NG * b + NG - 1)
                values_bias(0, (NG - 1) * GH * DC)
                heads_out(NG - 1)
                dve.wait_ge(v_ao, NG * b + NG)
                values_bias((NG - 1) * GH * DC, D)
                dve.wait_ge(pe_aT, 2 * b + 2)
                v.tensor_copy(aoT[:, 1, :], PS[:, 7, :]).then_inc(v_aT, 1)
                residual(pe_oC, 4, tg[:, 1:2], v_oC)

                layernorm(4 * b + 4, xw)
                with dve.If(b < B - 1):
                    evac_pa(b + 1, 0)
                    add_mask(b + 1, 2)
                evac_xT(4 * b + 4, both=True)
                dve.wait_ge(pe_gate, b + 1)
                v.tensor_tensor(lg[:], PS[:, 2, 0:QT * NE].rearrange("p (t e) -> p t e", t=QT),
                                bgD[:].unsqueeze(1).broadcast_to([P, QT, NE]), ALU.add).then_inc(v_lg, 1)
                dve.wait_ge(v_lg, b + 1)
                dve.nop(nofuse=True)
                for t in range(QT):
                    v.max(mx8[:, t, :], lg[:, t, :]).then_inc(*own.tick())
                dve.wait_ge(v_self, own.now())
                v.tensor_tensor(lgd[:], lg[:], mx8[:, :, 0:1].broadcast_to([P, QT, NE]),
                                ALU.subtract).then_inc(v_gd, 1)
                for t in range(QT):
                    v.max_index(ix8[:, t, :], mx8[:, t, :], lg[:, t, :]).then_inc(*own.tick())
                dve.wait_ge(v_self, own.now())
                v.tensor_copy(expert[:, bass.ds(QT * b, QT)], ix8[:, :, 0]).then_inc(*own.tick())
                with dve.If(b < B - 1):
                    rest_a(b + 1, 16 * b + 16)
                dve.wait_ge(a_ge, b + 1)
                v.tensor_reduce(ssum[:], lgd[:], AX.X, ALU.add).then_inc(*own.tick())
                dve.wait_ge(v_self, own.now())
                v.reciprocal(weight[:, bass.ds(QT * b, QT)], ssum[:]).then_inc(*own.tick())
                dve.wait_ge(v_self, own.now())
                dve.wait_ge(n_stored, 16 * b + 16)
                assert own.n == V_PER, own.n

            own.base, own.n = V_SET + V_PER * B, 0

            def alone(ins):
                ins.then_inc(*own.tick())
                dve.wait_ge(v_self, own.now())

            dve.wait_ge(g_set, 14)
            v.tensor_tensor(oh, expert[:].unsqueeze(2).broadcast_to([P, NT, NE]),
                            iota_e.unsqueeze(1).broadcast_to([P, NT, NE]), ALU.is_equal).then_inc(v_oh, 1)
            alone(v.tensor_scalar(weight[:], weight[:], tg[:, 3:4], None, ALU.mult))
            dve.wait_ge(pe_rank, 2)
            alone(v.tensor_copy(tot, PS[:, 1, 0:NT * NE].rearrange("p (t e) -> p t e", t=NT)))
            src, step_ = tot, 1
            n_pass = 0
            while step_ < NT:
                dst = inc[n_pass % 2]
                v.tensor_copy(dst[:, 0:step_, :], src[:, 0:step_, :]).then_inc(*own.tick())
                alone(v.tensor_tensor(dst[:, step_:, :], src[:, step_:, :], src[:, :NT - step_, :], ALU.add))
                src, step_, n_pass = dst, 2 * step_, n_pass + 1
            alone(v.tensor_copy(ncount, src[:, NT - 1, :]))
            alone(v.tensor_tensor(tot, src, tot, ALU.subtract))
            alone(v.tensor_tensor(tot, tot, PS[:, 0, 0:NT * NE].rearrange("p (t e) -> p t e", t=NT), ALU.add))
            alone(v.tensor_scalar(iota_k, iota_k, float(TS), None, ALU.mult))
            alone(v.tensor_tensor(cmp, ncount.unsqueeze(2).broadcast_to([P, NE, NE * 2]),
                                  iota_k.unsqueeze(1).broadcast_to([P, NE, NE * 2]), ALU.is_gt))
            alone(v.tensor_reduce(tiles, cmp, AX.X, ALU.add))
            tsrc, step_, n_pass = tiles, 1, 0
            while step_ < NE:
                dst = tinc[n_pass % 2]
                v.tensor_copy(dst[:, 0:step_], tsrc[:, 0:step_]).then_inc(*own.tick())
                alone(v.tensor_tensor(dst[:, step_:], tsrc[:, step_:], tsrc[:, :NE - step_], ALU.add))
                tsrc, step_, n_pass = dst, 2 * step_, n_pass + 1
            alone(v.tensor_tensor(tbase, tsrc, tiles, ALU.subtract))
            alone(v.tensor_scalar(tbase, tbase, float(TS), None, ALU.mult))
            alone(v.tensor_tensor(tcmp, tsrc.unsqueeze(1).broadcast_to([P, ET, NE]),
                                  iota_t.unsqueeze(2).broadcast_to([P, ET, NE]), ALU.is_le))
            alone(v.tensor_reduce(texf, tcmp, AX.X, ALU.add))
            v.tensor_scalar(tex, texf, float(NE - 1), None, ALU.min).then_inc(v_tex, 1)
            alone(v.tensor_tensor(tot, tot, tbase.unsqueeze(1).broadcast_to([P, NT, NE]), ALU.add))
            alone(v.tensor_tensor(tot, tot, oh, ALU.mult))
            alone(v.tensor_reduce(slotf, tot, AX.X, ALU.add))
            v.tensor_copy(slot, slotf).then_inc(v_slot, 1)

            def rows_in(j, par):
                dve.wait_ge(pe_xsT, j + 1)
                v.tensor_copy(xsT[par].rearrange("p k t -> p (k t)"), PS[:, par, :]).then_inc(v_xsT, 1)

            def rows_out(j, par, k, first=False):
                if not first:
                    dve.wait_ge(ys_stored[par], 16 * k)
                for t in range(2):
                    dve.wait_ge(pe_y, 2 * j + t + 1)
                    v.tensor_tensor(ys[par][:, t, :], PS[:, 6 + t, 0:D], b2[par], ALU.add).then_inc(v_y, 1)

            def pair(jj, first=False):
                rows_in(2 * jj + 1, 1)
                rows_out(2 * jj, 0, jj, first)
                rows_in(2 * jj + 2, 0)
                rows_out(2 * jj + 1, 1, jj, first)

            rows_in(0, 0)
            pair(0, True)
            with dve.Fori(1, ET // 2 - 1) as jj:
                pair(jj)
            rows_in(ET - 1, 1)
            rows_out(ET - 2, 0, ET // 2 - 1)
            rows_out(ET - 1, 1, ET // 2 - 1)
            for t in range(NT):
                bb = t // QT
                dve.wait_ge(gathered[bb], 16 * QT)
                dve.wait_ge(xr_loaded[bb % 2], 16 * (bb // 2 + 1))
                v.scalar_tensor_tensor(out=big[:, t, :], in0=big[:, t, :], scalar=weight[:, t:t + 1],
                                       in1=fin[bb % 2][:, t % QT, :], op0=ALU.mult, op1=ALU.add).then_inc(v_out, 1)


def kernel(**inputs):
    import concourse.bacc as bacc
    from concourse.bass_utils import run_bass_kernel_spmd as run
    import ml_dtypes

    i = {k: np.asarray(v) for k, v in inputs.items()}

    def t(x):
        return np.ascontiguousarray(x.swapaxes(-1, -2))

    qkv = np.stack([i["L0_ffn_Wq"], i["L0_ffn_Wk"], i["L0_ffn_Wv"]])
    arrays = {
        "x": i["x"],
        "ctx": i["ctx_1024"],
        "ctxT": t(i["ctx_1024"]),
        "A_mask": i["mask_BxSxS2_ff0"],
        "C_maskT": t(i["mask_1x1xSxS2_if1"][0, 0]),
        "g_x": i["g_xattn"],
        "g_f": i["g_ffn"],
        "A_WqWk": np.concatenate([i["L0_xattn_W_q"], i["L0_xattn_W_k"]], axis=1),
        "A_WvT": t(i["L0_xattn_W_v"]),
        "B_w": qkv.reshape(3, KD, P, HB, DB).transpose(3, 2, 0, 1, 4),
        "B_b": np.stack([i["L0_ffn_bq"], i["L0_ffn_bk"], i["L0_ffn_bv"]]).reshape(3, HB, DB).transpose(1, 2, 0),
        "B_Wr": i["L0_ffn_Wr"],
        "B_br": i["L0_ffn_br"][None],
        "B_Wo": i["L0_ffn_Wo"],
        "B_bo": i["L0_ffn_bo"],
        "C_WqT": t(i["L1_xattn_w_q"]),
        "C_WkT": t(i["L1_xattn_w_k"]),
        "C_WvT": t(i["L1_xattn_w_v"]),
        "C_WoT": t(i["L1_xattn_w_o"]),
        "C_bq": t(i["L1_xattn_b_q"].reshape(KD, P)),
        "C_bk": t(i["L1_xattn_b_k"].reshape(KD, P)),
        "C_bv": i["L1_xattn_b_v"],
        "C_bo": i["L1_xattn_b_o"],
        "D_wg": i["L1_ffn_w_gate"],
        "D_bg": i["L1_ffn_b_gate"],
        "D_W1": i["L1_ffn_W1"],
        "D_W2": i["L1_ffn_W2"],
        "D_b1": t(i["L1_ffn_b1"].reshape(NE, FM, P)),
        "D_b2": i["L1_ffn_b2"],
        "ones": np.ones((3, GH * C), ml_dtypes.bfloat16),
    }
    nc = bacc.Bacc("TRN2", target_bir_lowering=False, num_devices=1)
    feeds, aps = {}, {}
    for name, x in arrays.items():
        x = np.ascontiguousarray(x)
        feeds[f"in_{name}"] = x
        aps[name] = nc.dram_tensor(f"in_{name}", x.shape, mybir.dt.from_np(x.dtype), kind="ExternalInput").ap()
    aps["out"] = nc.dram_tensor("out", (B, S, D), F32, kind="ExternalOutput").ap()
    flamingo(nc, aps)
    r = run(nc, [feeds], core_ids=[0])
    return r.results[0]["out"]
```
